# Optimizing a Trainium2 kernel written in Bass

```python
import numpy as np
import jax
import jax.numpy as jnp

def _softmax(x, axis=-1):
    return jax.nn.softmax(x, axis=axis)

def _gelu(x):
    return jax.nn.gelu(x, approximate=True)

def _silu(x):
    return jax.nn.silu(x)

def _sigmoid(x):
    return jax.nn.sigmoid(x)

def _layernorm(x, axis=-1, eps=1e-05):
    m = jnp.mean(x, axis=axis, keepdims=True)
    v = jnp.var(x, axis=axis, keepdims=True)
    return (x - m) / jnp.sqrt(v + eps)

def _scatter_add(tgt, idx, src, axis=0):
    return tgt.at[idx].add(src)

def _segment_sum(src, seg, n):
    return jax.ops.segment_sum(src, seg, n)
kernel_name = 'mk_seq_preln_d1_jaxref_r2_5951fd'

def setup_inputs(seed: int=0):
    np.random.seed(seed)
    _w = jnp.asarray

    def _L0_attn_setup():
        import jax, jax.numpy as jnp
        import numpy as np
        THETA = 10000.0
        EPS = 1e-06
        N_HEADS = 16

        def apply_rope(x):
            b, h, l, d = x.shape
            inv_freq = 1.0 / THETA ** (jnp.arange(0, d, 2, dtype=jnp.float32) / d)
            t = jnp.arange(l, dtype=jnp.float32)
            freqs = t[:, None] * inv_freq[None, :]
            cos = jnp.cos(freqs)[None, None]
            sin = jnp.sin(freqs)[None, None]
            x1 = x[..., 0::2]
            x2 = x[..., 1::2]
            out = jnp.stack([x1 * cos - x2 * sin, x1 * sin + x2 * cos], axis=-1)
            return out.reshape(b, h, l, d)
        key = jax.random.key(seed)
        ks = jax.random.split(key, 5)
        dim = 512
        b, l = (1, 1024)
        scale = 1.0 / np.sqrt(dim)
        return {'x': jax.random.normal(ks[0], (b, l, dim), dtype=jnp.float32), 'wq': jax.random.normal(ks[1], (dim, dim), dtype=jnp.float32) * scale, 'wk': jax.random.normal(ks[2], (dim, dim), dtype=jnp.float32) * scale, 'wv': jax.random.normal(ks[3], (dim, dim), dtype=jnp.float32) * scale, 'wo': jax.random.normal(ks[4], (dim, dim), dtype=jnp.float32) * scale}
    _L0_attn_in = _L0_attn_setup()

    def _L0_ffn_setup():
        import jax, jax.numpy as jnp
        import numpy as np
        DIM = 512

        def _reference_tuple_inner(x, W_r, W_k, W_v, mu_r, mu_k):
            B, T, C = x.shape
            x_prev = jnp.concatenate([jnp.zeros((B, 1, C), x.dtype), x[:, :-1, :]], axis=1)
            xr = mu_r * x + (1.0 - mu_r) * x_prev
            xk = mu_k * x + (1.0 - mu_k) * x_prev
            r = jax.nn.sigmoid(jnp.einsum('btc,dc->btd', xr, W_r))
            k = jnp.einsum('btc,dc->btd', xk, W_k)
            k_act = jnp.square(jax.nn.relu(k))
            out = r * jnp.einsum('btc,dc->btd', k_act, W_v)
            new_state = x[:, -1, :]
            return (out, new_state)
        key = jax.random.key(seed)
        ks = jax.random.split(key, 6)
        B, T, C = (8, 1024, DIM)
        x = jax.random.normal(ks[0], (B, T, C), dtype=jnp.float32)
        s = 1.0 / np.sqrt(C)
        W_r = jax.random.uniform(ks[1], (C, C), jnp.float32, -s, s)
        W_k = jax.random.uniform(ks[2], (C, C), jnp.float32, -s, s)
        W_v = jax.random.uniform(ks[3], (C, C), jnp.float32, -s, s)
        mu_r = jax.random.uniform(ks[4], (C,), jnp.float32)
        mu_k = jax.random.uniform(ks[5], (C,), jnp.float32)
        return {'x': x, 'W_r': W_r, 'W_k': W_k, 'W_v': W_v, 'mu_r': mu_r, 'mu_k': mu_k}
    _L0_ffn_in = _L0_ffn_setup()
    _d = {'L0_attn_x': _L0_attn_in['x'], 'L0_attn_wq': _L0_attn_in['wq'], 'L0_attn_wk': _L0_attn_in['wk'], 'L0_attn_wv': _L0_attn_in['wv'], 'L0_attn_wo': _L0_attn_in['wo'], 'L0_ffn_W_r': _L0_ffn_in['W_r'], 'L0_ffn_W_k': _L0_ffn_in['W_k'], 'L0_ffn_W_v': _L0_ffn_in['W_v'], 'L0_ffn_mu_r': _L0_ffn_in['mu_r'], 'L0_ffn_mu_k': _L0_ffn_in['mu_k']}
    _x0 = _d['L0_attn_x']
    _d['L0_attn_x'] = jax.random.normal(jax.random.fold_in(jax.random.key(seed), 1), (4, 2048, 512), dtype=_x0.dtype)
    del _x0
    return _d

def reference(L0_attn_x, L0_attn_wq, L0_attn_wk, L0_attn_wv, L0_attn_wo, L0_ffn_W_r, L0_ffn_W_k, L0_ffn_W_v, L0_ffn_mu_r, L0_ffn_mu_k):

    def _L0_attn_ref(x, wq, wk, wv, wo):
        import jax, jax.numpy as jnp
        import numpy as np
        THETA = 10000.0
        EPS = 1e-06
        N_HEADS = 16

        def apply_rope(x):
            b, h, l, d = x.shape
            inv_freq = 1.0 / THETA ** (jnp.arange(0, d, 2, dtype=jnp.float32) / d)
            t = jnp.arange(l, dtype=jnp.float32)
            freqs = t[:, None] * inv_freq[None, :]
            cos = jnp.cos(freqs)[None, None]
            sin = jnp.sin(freqs)[None, None]
            x1 = x[..., 0::2]
            x2 = x[..., 1::2]
            out = jnp.stack([x1 * cos - x2 * sin, x1 * sin + x2 * cos], axis=-1)
            return out.reshape(b, h, l, d)
        b, l, dim = x.shape
        h = N_HEADS
        d = dim // h
        q = (x @ wq).reshape(b, l, h, d)
        k = (x @ wk).reshape(b, l, h, d)
        v = (x @ wv).reshape(b, l, h, d)
        q = apply_rope(q.transpose(0, 2, 1, 3)).transpose(0, 2, 1, 3)
        k = apply_rope(k.transpose(0, 2, 1, 3)).transpose(0, 2, 1, 3)
        Q = jax.nn.relu(q)
        K = jax.nn.relu(k)
        kv_state = jnp.einsum('blhd,blhm->blhdm', K, v)
        kv_cumsum = jnp.cumsum(kv_state, axis=1)
        k_cumsum = jnp.cumsum(K, axis=1)
        numerator = jnp.einsum('blhd,blhdm->blhm', Q, kv_cumsum)
        denominator = jnp.einsum('blhd,blhd->blh', Q, k_cumsum)[..., None]
        out = numerator / (denominator + EPS)
        out = out.reshape(b, l, dim)
        return out @ wo

    def _L0_ffn_ref(x, W_r, W_k, W_v, mu_r, mu_k):
        import jax, jax.numpy as jnp
        import numpy as np
        DIM = 512

        def _reference_tuple_inner(x, W_r, W_k, W_v, mu_r, mu_k):
            B, T, C = x.shape
            x_prev = jnp.concatenate([jnp.zeros((B, 1, C), x.dtype), x[:, :-1, :]], axis=1)
            xr = mu_r * x + (1.0 - mu_r) * x_prev
            xk = mu_k * x + (1.0 - mu_k) * x_prev
            r = jax.nn.sigmoid(jnp.einsum('btc,dc->btd', xr, W_r))
            k = jnp.einsum('btc,dc->btd', xk, W_k)
            k_act = jnp.square(jax.nn.relu(k))
            out = r * jnp.einsum('btc,dc->btd', k_act, W_v)
            new_state = x[:, -1, :]
            return (out, new_state)
        return _reference_tuple_inner(x, W_r, W_k, W_v, mu_r, mu_k)[0]
    x = L0_attn_x
    x = x + _L0_attn_ref(_layernorm(x, axis=-1), L0_attn_wq, L0_attn_wk, L0_attn_wv, L0_attn_wo)
    x = x + _L0_ffn_ref(_layernorm(x, axis=-1), L0_ffn_W_r, L0_ffn_W_k, L0_ffn_W_v, L0_ffn_mu_r, L0_ffn_mu_k)
    return x

_drawn_inputs = setup_inputs


def setup_inputs(seed=0):
    import zlib

    import numpy as np

    out = dict(_drawn_inputs(seed))
    spreads = {}
    factors = {'L0_ffn_W_r': 3.163, 'L0_ffn_mu_r': 6.481}
    for name, (base, spread) in spreads.items():
        noise = np.random.default_rng([zlib.crc32(name.encode()), seed]).standard_normal(out[name].shape)
        drawn = base * np.exp(spread * noise) if base else spread * noise
        out[name] = jnp.asarray(drawn.astype(out[name].dtype))
    for name, factor in factors.items():
        out[name] = (out[name] * factor).astype(out[name].dtype)
    return out
```

```python
from contextlib import ExitStack

import numpy as np

import concourse.bass as bass
from concourse import mybir

F32 = mybir.dt.float32
F32R = mybir.dt.float32r
ALU = mybir.AluOpType
ACT = mybir.ActivationFunctionType
AX_X = mybir.AxisListType.X

P = 128
C = 512
KB = C // P
H = 16
D = C // H
HG = P // D
G = H // HG
UNROLL = 4
LN_EPS = 1e-5
DEN_EPS = 1e-6


def attention_phase(nc, sem, x, wq, wk, wv, wo, tables, mask, tri, eye, x1_dram, ffn_raw, ffn_w):
    B, L, _ = x.shape
    tiles = B * L // P
    per_batch = L // P
    inner = per_batch // UNROLL
    x_tiles = x.rearrange("b (n p) c -> (b n) p c", p=P)
    x1_tiles = x1_dram.rearrange("(n p) c -> n p c", p=P)

    with ExitStack() as ctx:
        def sb(name, shape, dt=F32):
            return ctx.enter_context(nc.sbuf_tensor(name, shape, dt))

        def bank(name):
            return ctx.enter_context(nc.psum_tensor(name, [P, 512], F32))

        w_dram = [wk, wq, wv, wo]
        w_hi = [sb(f"w_hi{i}", [P, KB, C], F32R) for i in range(4)]
        w_lo = [sb(f"w_lo{i}", [P, KB, C], F32R) for i in range(4)]
        WK, WQ, WV, WO = range(4)
        table_sb = sb("table_sb", [P, per_batch + 1, 2 * D])
        mask_sb = sb("mask_sb", [P, P])
        eye_sb = sb("eye_sb", [P, P])
        tri_sb = sb("tri_sb", [P, 2 * P])
        tri_r = sb("tri_r", [P, 2 * P], F32R)
        zeros_r = sb("zeros_r", [P, C], F32R)
        power, epsilon, three_halves = sb("power", [P, 1]), sb("epsilon", [P, 1]), sb("three_halves", [P, 1])
        x_sb = [sb(f"x_sb{u}", [P, C]) for u in range(UNROLL)]
        stats = [sb(f"stats{u}", [P, 6]) for u in range(2)]
        mean_var = [sb(f"mean_var{u}", [P, 2]) for u in range(2)]
        rstd = [sb(f"rstd{u}", [P, 4]) for u in range(2)]
        xn = sb("xn", [P, C])
        xnT_hi = [sb(f"xnT_hi{u}", [P, KB, P], F32R) for u in range(2)]
        xnT_lo = [sb(f"xnT_lo{u}", [P, KB, P], F32R) for u in range(2)]
        k_cos, k_sin, k_sum = sb("k_cos", [P, C]), sb("k_sin", [P, C]), sb("k_sum", [P, C])
        q_cos, q_sin, q_sum = sb("q_cos", [P, C]), sb("q_sin", [P, C]), sb("q_sum", [P, C])
        k_nat = [sb(f"k_nat{u}", [P, C]) for u in range(2)]
        k_hi, k_lo = sb("k_hi", [P, C], F32R), sb("k_lo", [P, C], F32R)
        q_nat, q_norm, v_nat = sb("q_nat", [P, C]), sb("q_norm", [P, C]), sb("v_nat", [P, C])
        prod = sb("prod", [P, C])
        den = sb("den", [P, 3, H])
        kT_hi, kT_lo = sb("kT_hi", [P, G, P], F32R), sb("kT_lo", [P, G, P], F32R)
        qT = sb("qT", [P, G, P])
        qx_hi, qx_lo = sb("qx_hi", [P, G, HG, P], F32R), sb("qx_lo", [P, G, HG, P], F32R)
        probs = sb("probs", [P, G, HG * P])
        state = sb("state", [P, G, P])
        oT_hi, oT_lo = sb("oT_hi", [P, G, P], F32R), sb("oT_lo", [P, G, P], F32R)

        bank0, bank1, bank2, bank3 = bank("bank0"), bank("bank1"), bank("bank2"), bank("bank3")
        bank4, bank5, kcum, kv = bank("bank4"), bank("bank5"), bank("kcum"), bank("kv")
        xnT_ps, outT_ps = bank0, bank0
        attn_ps = bank1
        kT_ps, qT_ps = bank2, bank5
        k_ps, v_ps, q_ps = bank3, bank3, bank4
        score_ps = [bank0, bank1, bank2, bank5]

        consts_loaded, table_loaded, ffn_loaded = sem("consts_loaded"), sem("table_loaded"), sem("ffn_loaded")
        w_loaded = [sem(f"w_loaded{i}") for i in range(4)]
        w_hi_ready, w_lo_ready = sem("w_hi_ready"), sem("w_lo_ready")
        tri_ready, consts_set, zeros_set = sem("tri_ready"), sem("consts_set"), sem("zeros_set")
        x_loaded = [sem(f"x_loaded{u}") for u in range(UNROLL)]
        x1_stored = [sem(f"x1_stored{u}") for u in range(UNROLL)]
        stats_done, meanvar_ready, rstd_ready = sem("stats_done"), sem("meanvar_ready"), sem("rstd_ready")
        rstd_step = sem("rstd_step")
        xn_ready = sem("xn_ready")
        xnT_in_psum, xnT_hi_ready, xnT_ready = sem("xnT_in_psum"), sem("xnT_hi_ready"), sem("xnT_ready")
        k_in_psum, q_in_psum, v_in_psum = sem("k_in_psum"), sem("q_in_psum"), sem("v_in_psum")
        k_rotated, q_rotated = sem("k_rotated"), sem("q_rotated")
        k_summed, q_summed = sem("k_summed"), sem("q_summed")
        k_ready, k_hi_ready, k_split, k_split_used = sem("k_ready"), sem("k_hi_ready"), sem("k_split"), sem("k_split_used")
        q_ready, v_ready = sem("q_ready"), sem("v_ready")
        kcum_ready, kcum_used = sem("kcum_ready"), sem("kcum_used")
        den_summed, den_guarded, den_inverted, q_normed = sem("den_summed"), sem("den_guarded"), sem("den_inverted"), sem("q_normed")
        kT_in_psum, kT_hi_ready, kT_ready = sem("kT_in_psum"), sem("kT_hi_ready"), sem("kT_ready")
        qT_in_psum, qx_ready = sem("qT_in_psum"), sem("qx_ready")
        qx_hi_ready = [sem(f"qx_hi_ready{q}") for q in range(HG)]
        kv_ready, state_ready = sem("kv_ready"), sem("state_ready")
        scores_ready = [sem(f"scores_ready{g}") for g in range(G)]
        scores_free = [sem(f"scores_free{g}") for g in range(G)]
        outT_in_psum, oT_hi_ready, oT_ready = sem("outT_in_psum"), sem("oT_hi_ready"), sem("oT_ready")
        attn_ready, x1_ready = sem("attn_ready"), sem("x1_ready")

        block = ctx.enter_context(nc.Block())

        def heads(ap):
            return ap.rearrange("p (h d) -> p h d", d=D)

        raw = [ffn_raw[0][:, :, :], ffn_raw[1][:, :, :], ffn_raw[2][:, :, :], probs[:, :, :]]

        def split3(psum, lhs_hi, lhs_lo, rhs_hi, rhs_lo, start, stop):
            nc.tensor.matmul(psum, lhs_hi, rhs_hi, start=start, stop=False)
            nc.tensor.matmul(psum, lhs_lo, rhs_hi, start=False, stop=False)
            return nc.tensor.matmul(psum, lhs_hi, rhs_lo, start=False, stop=stop)

        @block.sync
        def _(sp):
            sp.dma_start(x_sb[0][:], x_tiles[0, :, :]).then_inc(x_loaded[0], 16)
            for dst, src in ((eye_sb, eye), (tri_sb, tri), (mask_sb, mask)):
                sp.dma_start(dst[:], src).then_inc(consts_loaded, 16)
            for i in (WK, WQ):
                sp.dma_start(raw[i], w_dram[i].rearrange("(k p) n -> p k n", p=P)).then_inc(w_loaded[i], 16)
            sp.dma_start(table_sb[:, :, :], tables).then_inc(table_loaded, 16)
            for u in range(1, UNROLL):
                sp.dma_start(x_sb[u][:], x_tiles[u, :, :]).then_inc(x_loaded[u], 16)
            for i in (WV, WO):
                sp.dma_start(raw[i], w_dram[i].rearrange("(k p) n -> p k n", p=P)).then_inc(w_loaded[i], 16)
            sp.wait_ge(w_lo_ready, 3)
            for i in range(3):
                sp.dma_start(ffn_raw[i][:, :, :], ffn_w[i].rearrange("(k p) n -> p k n", p=P)).then_inc(ffn_loaded, 16)

            def store(tile, turn, u):
                sp.wait_ge(x1_ready, tile + 2)
                sp.dma_start(x1_tiles[bass.ds(tile, 1), :, :].rearrange("o p c -> (o p) c"),
                             x_sb[u][:]).then_inc(x1_stored[u], 16)
                sp.wait_ge(x1_stored[u], 16 * turn + 16)

            with sp.Fori(0, tiles // UNROLL - 1) as turn:
                for u in range(UNROLL):
                    tile = turn * UNROLL + u
                    store(tile, turn, u)
                    sp.dma_start(x_sb[u][:], x_tiles[bass.ds(tile + UNROLL, 1), :, :].rearrange("o p c -> (o p) c")).then_inc(x_loaded[u], 16)
            for u in range(UNROLL):
                store(tiles - UNROLL + u, tiles // UNROLL - 1, u)
                if u < 2:
                    sp.dma_start(x_sb[u][:], x_tiles[u, :, :]).then_inc(x_loaded[u], 16)
            for u in range(2):
                sp.wait_ge(x_loaded[u], 16 * (tiles // UNROLL) + 16)
            sp.wait_ge(ffn_loaded, 48)

        @block.tensor
        def _(pe):
            def transpose_xn(slot):
                for k in range(KB):
                    last = nc.tensor.transpose(xnT_ps[:, k * P:(k + 1) * P], xn[:, k * P:(k + 1) * P], eye_sb[:])
                last.then_inc(xnT_in_psum, 1)

            def project(psum, slot, w, done):
                for k in range(KB):
                    last = split3(psum[:], xnT_hi[slot][:, k, :], xnT_lo[slot][:, k, :],
                                  w_hi[w][:, k, :], w_lo[w][:, k, :], k == 0, k == KB - 1)
                last.then_inc(done, 1)

            def step(tile, u):
                ahead, here = (u + 1) % 2, u % 2
                pe.wait_ge(xn_ready, tile + 2)
                pe.wait_ge(oT_ready, tile + 1)
                transpose_xn(ahead)
                pe.wait_ge(k_ready, tile + 1)
                pe.wait_ge(scores_free[2], tile + 1)
                for g in range(G):
                    last = nc.tensor.transpose(kT_ps[:, g * P:(g + 1) * P], k_nat[here][:, g * P:(g + 1) * P], eye_sb[:])
                last.then_inc(kT_in_psum, 1)
                pe.wait_ge(k_split, tile + 1)
                nc.tensor.matmul(kcum[:], tri_r[:, 0:P], k_hi[:], start=False, stop=False, skip_group_check=True)
                nc.tensor.matmul(kcum[:], tri_r[:, 0:P], k_lo[:], start=False, stop=True,
                                 skip_group_check=True).then_inc(kcum_ready, 1)
                pe.wait_ge(xnT_ready, tile + 2)
                pe.wait_ge(v_ready, tile + 1)
                project(k_ps, ahead, WK, k_in_psum)
                pe.wait_ge(kcum_used, tile + 1)
                nc.tensor.matmul(kcum[:], tri_r[:, P:2 * P], k_hi[:], start=False, stop=False, skip_group_check=True)
                nc.tensor.matmul(kcum[:], tri_r[:, P:2 * P], k_lo[:], start=False, stop=True,
                                 skip_group_check=True).then_inc(k_split_used, 1)
                pe.wait_ge(q_normed, tile + 1)
                pe.wait_ge(scores_free[3], tile + 1)
                for g in range(G):
                    last = nc.tensor.transpose(qT_ps[:, g * P:(g + 1) * P], q_norm[:, g * P:(g + 1) * P], eye_sb[:])
                last.then_inc(qT_in_psum, 1)
                pe.wait_ge(q_rotated, tile + 1)
                project(q_ps, ahead, WQ, q_in_psum)
                pe.wait_ge(kT_ready, tile + 1)
                pe.wait_ge(qx_ready, tile + 1)
                pe.wait_ge(x1_ready, tile + 1)
                for g in range(G):
                    split3(score_ps[g][:], kT_hi[:, g, :], kT_lo[:, g, :],
                           qx_hi[:, g, :, :].rearrange("p a b -> p (a b)"),
                           qx_lo[:, g, :, :].rearrange("p a b -> p (a b)"), True, True).then_inc(scores_ready[g], 1)
                pe.wait_ge(state_ready, tile + 1)
                for g in range(G):
                    last = nc.tensor.matmul(kv[:, g * P:(g + 1) * P], k_nat[here][:, g * P:(g + 1) * P],
                                            v_nat[:, g * P:(g + 1) * P], start=False, stop=True, skip_group_check=True)
                last.then_inc(kv_ready, 1)
                pe.wait_ge(scores_free[0], tile + 2)
                for g in range(G):
                    nc.tensor.matmul(outT_ps[:, g * P:(g + 1) * P], state[:, g, :], qT[:, g, :],
                                     start=(g == 0), stop=False, skip_group_check=True)
                for g in range(G):
                    pe.wait_ge(scores_free[g], tile + 2)
                    for h in range(HG):
                        f = g * P + h * D
                        last = nc.tensor.matmul(outT_ps[h * D:(h + 1) * D, g * P:(g + 1) * P], v_nat[:, f:f + D],
                                                probs[:, g, h * P:(h + 1) * P], start=False,
                                                stop=(g == G - 1 and h == HG - 1), skip_group_check=True)
                last.then_inc(outT_in_psum, 1)
                pe.wait_ge(k_rotated, tile + 2)
                project(v_ps, ahead, WV, v_in_psum)
                pe.wait_ge(oT_ready, tile + 2)
                for g in range(G):
                    last = split3(attn_ps[:], oT_hi[:, g, :], oT_lo[:, g, :], w_hi[WO][:, g, :], w_lo[WO][:, g, :],
                                  g == 0, g == G - 1)
                last.then_inc(attn_ready, 1)

            pe.wait_ge(consts_loaded, 48)
            pe.wait_ge(consts_set, 1)
            pe.wait_ge(tri_ready, 1)
            pe.wait_ge(xn_ready, 1)
            transpose_xn(0)
            pe.wait_ge(xnT_ready, 1)
            pe.wait_ge(w_lo_ready, 1)
            project(k_ps, 0, WK, k_in_psum)
            pe.wait_ge(w_lo_ready, 2)
            project(q_ps, 0, WQ, q_in_psum)
            pe.wait_ge(w_lo_ready, 3)
            pe.wait_ge(k_rotated, 1)
            project(v_ps, 0, WV, v_in_psum)
            pe.wait_ge(w_lo_ready, 4)
            with pe.Fori(0, B) as b:
                nc.tensor.matmul(kcum[:], zeros_r[:, 0:P], zeros_r[:], start=True, stop=True, skip_group_check=True)
                nc.tensor.matmul(kv[:], zeros_r[:, 0:P], zeros_r[:], start=True, stop=True,
                                 skip_group_check=True).then_inc(kv_ready, 1)
                with pe.Fori(0, inner) as turn:
                    for u in range(UNROLL):
                        step(b * per_batch + turn * UNROLL + u, u)

        @block.scalar
        def _(act):
            def xnT_high(slot, count):
                act.wait_ge(xnT_in_psum, count)
                nc.scalar.copy(xnT_hi[slot][:, :, :].rearrange("p k n -> p (k n)"), xnT_ps[:]).then_inc(xnT_hi_ready, 1)

            def keys(slot, count):
                act.wait_ge(k_summed, count)
                nc.scalar.activation(k_nat[slot][:], k_sum[:], ACT.Relu).then_inc(k_ready, 1)
                act.wait_ge(k_ready, count)
                nc.scalar.copy(k_hi[:], k_nat[slot][:]).then_inc(k_hi_ready, 1)

            def queries(count):
                act.wait_ge(q_summed, count)
                nc.scalar.activation(q_nat[:], q_sum[:], ACT.Relu).then_inc(q_ready, 1)

            def values(count):
                act.wait_ge(v_in_psum, count)
                nc.scalar.copy(v_nat[:], v_ps[:]).then_inc(v_ready, 1)

            def step(b, tile, u):
                xnT_high((u + 1) % 2, tile + 2)
                act.wait_ge(kT_in_psum, tile + 1)
                nc.scalar.copy(kT_hi[:, :, :].rearrange("p g n -> p (g n)"), kT_ps[:]).then_inc(kT_hi_ready, 1)
                act.wait_ge(kv_ready, tile + b + 1)
                for q in range(HG):
                    own = slice(q * D, (q + 1) * D)
                    last = nc.scalar.copy(state[own, :, own], kv[own, :].rearrange("p (g n) -> p g n", g=G)[:, :, own])
                last.then_inc(state_ready, 1)
                act.wait_ge(qT_in_psum, tile + 1)
                nc.scalar.copy(qT[:, :, :].rearrange("p g n -> p (g n)"), qT_ps[:])
                for q in range(HG):
                    own = slice(q * D, (q + 1) * D)
                    nc.scalar.copy(qx_hi[own, :, q, :], qT_ps[own, :].rearrange("p (g n) -> p g n", g=G)).then_inc(qx_hi_ready[q], 1)
                act.wait_ge(k_split_used, tile + 1)
                keys((u + 1) % 2, tile + 2)
                act.wait_ge(q_normed, tile + 1)
                queries(tile + 2)
                act.wait_ge(outT_in_psum, tile + 1)
                nc.scalar.copy(oT_hi[:, :, :].rearrange("p g n -> p (g n)"), outT_ps[:]).then_inc(oT_hi_ready, 1)
                values(tile + 2)

            for i in (WK, WQ, WV, WO):
                act.wait_ge(w_loaded[i], 16)
                nc.scalar.copy(w_hi[i][:, :, :], raw[i]).then_inc(w_hi_ready, 1)
                if i == WK:
                    act.wait_ge(consts_loaded, 48)
                    nc.scalar.copy(tri_r[:], tri_sb[:]).then_inc(tri_ready, 1)
                    xnT_high(0, 1)
            keys(0, 1)
            queries(1)
            values(1)
            act.wait_ge(consts_set, 1)
            act.wait_ge(zeros_set, 1)
            with act.Fori(0, B) as b:
                with act.Fori(0, inner) as turn:
                    for u in range(UNROLL):
                        step(b, b * per_batch + turn * UNROLL + u, u)

        @block.vector
        def _(dve):
            def normalize_stats(slot, loads):
                dve.wait_ge(x_loaded[slot], loads)
                nc.vector.bn_stats(stats[slot % 2][:], x_sb[slot][:]).then_inc(stats_done, 1)

            def mean_and_variance(slot):
                nc.vector.bn_aggr(mean_var[slot % 2][:], stats[slot % 2][:]).then_inc(meanvar_ready, 1)

            def normalize(slot, count):
                dve.wait_ge(rstd_ready, count)
                nc.vector.tensor_scalar(xn[:], x_sb[slot][:], mean_var[slot % 2][:, 0:1], rstd[slot % 2][:, 3:4],
                                        ALU.subtract, ALU.mult).then_inc(xn_ready, 1)

            def xnT_low(slot, count):
                dve.wait_ge(xnT_hi_ready, count)
                nc.vector.tensor_tensor(xnT_lo[slot][:, :, :].rearrange("p k n -> p (k n)"), xnT_ps[:],
                                        xnT_hi[slot][:, :, :].rearrange("p k n -> p (k n)").bitcast(F32),
                                        ALU.subtract).then_inc(xnT_ready, 1)

            def rotate(psum, by_cos, by_sin, position, done):
                pair = table_sb[:, bass.ds(position, 1), :] if not isinstance(position, int) else table_sb[:, position:position + 1, :]
                cos = pair[:, :, 0:D].broadcast_to([P, H, D])
                sin = pair[:, :, D:2 * D].rearrange("p o (f c) -> p o f c", c=2).broadcast_to([P, H, D // 2, 2])
                nc.vector.tensor_tensor(heads(by_cos[:]), heads(psum[:]), cos, ALU.mult)
                swapped = psum[:].rearrange("p (h f c) -> p h f c", h=H, c=2)[:, :, :, ::-1]
                nc.vector.tensor_tensor(by_sin[:].rearrange("p (h f c) -> p h f c", h=H, c=2), swapped, sin,
                                        ALU.mult).then_inc(done, 1)

            def step(turn, tile, all_turn, u):
                xnT_low((u + 1) % 2, tile + 2)
                dve.wait_ge(q_ready, tile + 1)
                dve.wait_ge(kcum_ready, tile + 1)
                nc.vector.tensor_tensor(prod[:], q_nat[:], kcum[:], ALU.mult).then_inc(kcum_used, 1)
                dve.wait_ge(kcum_used, tile + 1)
                nc.vector.tensor_reduce(den[:, 0, :], heads(prod[:]), AX_X, ALU.add).then_inc(den_summed, 1)
                dve.wait_ge(den_summed, tile + 1)
                nc.vector.tensor_scalar_add(den[:, 1, :], den[:, 0, :], DEN_EPS).then_inc(den_guarded, 1)
                dve.wait_ge(den_guarded, tile + 1)
                nc.vector.reciprocal(den[:, 2, :], den[:, 1, :]).then_inc(den_inverted, 1)
                dve.wait_ge(den_inverted, tile + 1)
                nc.vector.tensor_tensor(heads(q_norm[:]), heads(q_nat[:]),
                                        den[:, 2, :].rearrange("p (h o) -> p h o", o=1).broadcast_to([P, H, D]),
                                        ALU.mult).then_inc(q_normed, 1)
                dve.wait_ge(kT_hi_ready, tile + 1)
                nc.vector.tensor_tensor(kT_lo[:, :, :].rearrange("p g n -> p (g n)"), kT_ps[:],
                                        kT_hi[:, :, :].rearrange("p g n -> p (g n)").bitcast(F32),
                                        ALU.subtract).then_inc(kT_ready, 1)
                dve.wait_ge(k_in_psum, tile + 2)
                dve.wait_ge(k_summed, tile + 1)
                rotate(k_ps, k_cos, k_sin, turn * UNROLL + u + 1, k_rotated)
                ahead = (u + 2) % UNROLL
                normalize_stats(ahead, 16 * all_turn + (16 if u < 2 else 32))
                dve.wait_ge(stats_done, tile + 3)
                for q in range(HG):
                    own = slice(q * D, (q + 1) * D)
                    dve.wait_ge(qx_hi_ready[q], tile + 1)
                    last = nc.vector.tensor_tensor(qx_lo[own, :, q, :], qT_ps[own, :].rearrange("p (g n) -> p g n", g=G),
                                                   qx_hi[own, :, q, :].bitcast(F32), ALU.subtract)
                last.then_inc(qx_ready, 1)
                mean_and_variance(ahead)
                dve.wait_ge(q_in_psum, tile + 2)
                dve.wait_ge(q_summed, tile + 1)
                rotate(q_ps, q_cos, q_sin, turn * UNROLL + u + 1, q_rotated)
                for g in range(G):
                    dve.wait_ge(scores_ready[g], tile + 1)
                    nc.vector.tensor_tensor(probs[:, g, :].rearrange("p (h n) -> p h n", h=HG),
                                            score_ps[g][:].rearrange("p (h n) -> p h n", h=HG),
                                            mask_sb[:].rearrange("p (o n) -> p o n", o=1).broadcast_to([P, HG, P]),
                                            ALU.mult).then_inc(scores_free[g], 1)
                normalize(ahead, tile + 3)
                dve.wait_ge(oT_hi_ready, tile + 1)
                nc.vector.tensor_tensor(oT_lo[:, :, :].rearrange("p g n -> p (g n)"), outT_ps[:],
                                        oT_hi[:, :, :].rearrange("p g n -> p (g n)").bitcast(F32),
                                        ALU.subtract).then_inc(oT_ready, 1)
                dve.wait_ge(attn_ready, tile + 1)
                nc.vector.tensor_tensor(x_sb[u][:], x_sb[u][:], attn_ps[:], ALU.add).then_inc(x1_ready, 1)

            nc.vector.memset(power[:], -0.5)
            nc.vector.memset(epsilon[:], LN_EPS)
            nc.vector.memset(three_halves[:], 1.5)
            nc.vector.memset(state[:, :, :], 0.0)
            nc.vector.memset(zeros_r[:].bitcast(F32), 0.0).then_inc(consts_set, 1)
            normalize_stats(0, 16)
            dve.wait_ge(stats_done, 1)
            mean_and_variance(0)
            normalize_stats(1, 16)
            dve.wait_ge(stats_done, 2)
            mean_and_variance(1)
            normalize(0, 1)
            for free in (oT_ready, x1_ready, *scores_free):
                dve.sem_inc(free, 1)
            for i in (WK, WQ, WV, WO):
                dve.wait_ge(w_hi_ready, i + 1)
                nc.vector.tensor_tensor(w_lo[i][:, :, :], raw[i], w_hi[i][:, :, :].bitcast(F32),
                                        ALU.subtract).then_inc(w_lo_ready, 1)
                if i == WK:
                    xnT_low(0, 1)
                    normalize(1, 2)
                if i == WQ:
                    dve.wait_ge(table_loaded, 16)
                    dve.wait_ge(k_in_psum, 1)
                    rotate(k_ps, k_cos, k_sin, 0, k_rotated)
            dve.wait_ge(q_in_psum, 1)
            rotate(q_ps, q_cos, q_sin, 0, q_rotated)
            dve.wait_ge(zeros_set, 1)
            with dve.Fori(0, B) as b:
                with dve.Fori(0, inner) as turn:
                    for u in range(UNROLL):
                        step(turn, b * per_batch + turn * UNROLL + u, b * inner + turn + 0, u)

        @block.gpsimd
        def _(pool):
            def inverse_deviation(slot, count):
                r = rstd[slot]
                pool.wait_ge(meanvar_ready, count)
                nc.gpsimd.tensor_tensor(r[:, 0:1], mean_var[slot][:, 1:2], epsilon[:], ALU.add).then_inc(rstd_step, 1)
                pool.wait_ge(rstd_step, 6 * count - 5)
                nc.gpsimd.tensor_tensor(r[:, 1:2], r[:, 0:1], power[:], ALU.pow).then_inc(rstd_step, 1)
                pool.wait_ge(rstd_step, 6 * count - 4)
                nc.gpsimd.tensor_tensor(r[:, 2:3], r[:, 1:2], r[:, 1:2], ALU.mult).then_inc(rstd_step, 1)
                pool.wait_ge(rstd_step, 6 * count - 3)
                nc.gpsimd.tensor_tensor(r[:, 2:3], r[:, 2:3], r[:, 0:1], ALU.mult).then_inc(rstd_step, 1)
                pool.wait_ge(rstd_step, 6 * count - 2)
                nc.gpsimd.tensor_tensor(r[:, 2:3], r[:, 2:3], power[:], ALU.mult).then_inc(rstd_step, 1)
                pool.wait_ge(rstd_step, 6 * count - 1)
                nc.gpsimd.tensor_tensor(r[:, 2:3], r[:, 2:3], three_halves[:], ALU.add).then_inc(rstd_step, 1)
                pool.wait_ge(rstd_step, 6 * count)
                nc.gpsimd.tensor_tensor(r[:, 3:4], r[:, 2:3], r[:, 1:2], ALU.mult).then_inc(rstd_ready, 1)

            def keys(count):
                pool.wait_ge(k_rotated, count)
                nc.gpsimd.tensor_tensor(k_sum[:], k_cos[:], k_sin[:], ALU.add).then_inc(k_summed, 1)

            def queries(count):
                pool.wait_ge(q_rotated, count)
                nc.gpsimd.tensor_tensor(q_sum[:], q_cos[:], q_sin[:], ALU.add).then_inc(q_summed, 1)

            def keys_low(slot, count):
                pool.wait_ge(k_hi_ready, count)
                nc.gpsimd.tensor_tensor(k_lo[:], k_nat[slot][:], k_hi[:].bitcast(F32), ALU.subtract).then_inc(k_split, 1)

            def step(tile, u):
                pool.wait_ge(k_ready, tile + 1)
                keys(tile + 2)
                inverse_deviation(u % 2, tile + 3)
                pool.wait_ge(q_ready, tile + 1)
                queries(tile + 2)
                keys_low((u + 1) % 2, tile + 2)

            pool.wait_ge(consts_set, 1)
            inverse_deviation(0, 1)
            inverse_deviation(1, 2)
            nc.gpsimd.memset(qx_hi[:, :, :, :].bitcast(F32), 0.0)
            nc.gpsimd.memset(qx_lo[:, :, :, :].bitcast(F32), 0.0).then_inc(zeros_set, 1)
            keys(1)
            queries(1)
            keys_low(0, 1)
            with pool.Fori(0, B) as b:
                with pool.Fori(0, inner) as turn:
                    for u in range(UNROLL):
                        step(b * per_batch + turn * UNROLL + u, u)


def mix_phase(nc, sem, x1_dram, w_raw, mu, eye, out, blocks_per_batch):
    T = 512
    J = T // P
    N = blocks_per_batch
    blocks = x1_dram.shape[0] // T
    B = blocks // N
    x1_blocks = x1_dram.rearrange("(n j p) c -> n p j c", p=P, j=J)
    out_tiles = out.rearrange("b (n p) c -> (b n) p c", p=P)

    with ExitStack() as ctx:
        def sb(name, shape, dt=F32):
            return ctx.enter_context(nc.sbuf_tensor(name, shape, dt))

        WR, WK, WV = range(3)
        w_hi = [sb(f"f_hi{i}", [P, KB, C], F32R) for i in range(3)]
        w_lo = [sb(f"f_lo{i}", [P, KB, C], F32R) for i in range(3)]
        mu_sb = sb("mu_sb", [P, 2, KB])
        rest_sb = sb("rest_sb", [P, 2, KB])
        eye_sb = sb("f_eye", [P, P])
        power, epsilon, three_halves = sb("f_power", [P, J]), sb("f_epsilon", [P, J]), sb("f_three_halves", [P, J])
        x1_sb = [sb(f"x1_sb{i}", [P, J, C]) for i in range(2)]
        stats = sb("f_stats", [P, J, 6])
        mean_var = sb("f_mean_var", [P, J, 2])
        rstd = sb("f_rstd", [P, 4, J])
        xn = sb("f_xn", [P, J, C])
        xT = sb("xT", [P, KB, T + 1])
        part = [[sb(f"part{m}{i}", [P, T]) for i in range(2)] for m in range(2)]
        mixed = [[sb(f"mixed{m}{i}", [P, T]) for i in range(2)] for m in range(2)]
        m_hi = [sb(f"m_hi{m}", [P, KB, T], F32R) for m in range(2)]
        m_lo = [sb(f"m_lo{m}", [P, KB, T], F32R) for m in range(2)]
        k_relu = [sb(f"k_relu{i}", [P, T]) for i in range(2)]
        k_square = [sb(f"k_square{i}", [P, T]) for i in range(2)]
        ka_hi, ka_lo = sb("ka_hi", [P, KB, T], F32R), sb("ka_lo", [P, KB, T], F32R)
        gate = sb("gate", [P, J, C])
        gated = [sb(f"gated{i}", [P, C]) for i in range(2)]
        result = [sb(f"result{i}", [P, C]) for i in range(2)]

        xT_ps = [ctx.enter_context(nc.psum_tensor(f"xT_ps{i}", [P, 512], F32)) for i in range(2)]
        k_ps = [ctx.enter_context(nc.psum_tensor(f"f_k_ps{i}", [P, 512], F32)) for i in range(2)]
        r_ps = [ctx.enter_context(nc.psum_tensor(f"f_r_ps{i}", [P, 512], F32)) for i in range(2)]
        v_ps = [ctx.enter_context(nc.psum_tensor(f"f_v_ps{i}", [P, 512], F32)) for i in range(2)]

        consts_loaded, consts_set, rest_ready = sem("f_consts_loaded"), sem("f_consts_set"), sem("rest_ready")
        w_hi_ready, w_lo_ready = sem("f_w_hi_ready"), sem("f_w_lo_ready")
        x1_loaded = [sem(f"x1_loaded{i}") for i in range(2)]
        stats_done, meanvar_ready = sem("f_stats_done"), sem("f_meanvar_ready")
        rstd_step = sem("f_rstd_step")
        rstd_ready, xn_ready = sem("f_rstd_ready"), sem("f_xn_ready")
        carried = sem("carried")
        def sems(name):
            return [sem(f"{name}{i}") for i in range(4)]
        xT_in_psum, xT_ready = sems("xT_in_psum"), sems("xT_ready")
        part_ready, mixed_ready = [sem("part_r"), sem("part_k")], [sem("mixed_r"), sem("mixed_k")]
        m_hi_ready, m_ready = [sem("m_hi_r"), sem("m_hi_k")], [sems("m_r"), sems("m_k")]
        k_in_psum, relu_done, square_done, ka_hi_ready, ka_ready = sems("f_k_in_psum"), sems("relu_done"), sems("square_done"), sems("ka_hi_ready"), sems("ka_ready")
        r_in_psum, gate_ready, v_in_psum, gated_ready, result_ready = sems("r_in_psum"), sems("gate_ready"), sems("f_v_in_psum"), sems("gated_ready"), sems("result_ready")
        stored = sems("stored")

        block = ctx.enter_context(nc.Block())

        def split3(psum, lhs_hi, lhs_lo, rhs_hi, rhs_lo, start, stop):
            nc.tensor.matmul(psum, lhs_hi, rhs_hi, start=start, stop=False)
            nc.tensor.matmul(psum, lhs_lo, rhs_hi, start=False, stop=False)
            return nc.tensor.matmul(psum, lhs_hi, rhs_lo, start=False, stop=stop)

        @block.sync
        def _(sp):
            sp.dma_start(x1_sb[0][:, :, :], x1_blocks[0, :, :, :]).then_inc(x1_loaded[0], 16)
            sp.dma_start(mu_sb[:, :, :], mu).then_inc(consts_loaded, 16)
            sp.dma_start(eye_sb[:], eye).then_inc(consts_loaded, 16)
            sp.dma_start(x1_sb[1][:, :, :], x1_blocks[1, :, :, :]).then_inc(x1_loaded[1], 16)

            def store(n, j):
                sp.wait_ge(result_ready[j], n + 1 + (j >= 2))
                sp.dma_start(out_tiles[bass.ds(n * J + j, 1), :, :].rearrange("o p c -> (o p) c"), result[j % 2][:]).then_inc(stored[j], 16)

            with sp.Fori(0, blocks // 2 - 1) as pair:
                for i in range(2):
                    n = pair * 2 + i
                    for j in range(J):
                        store(n, j)
                    sp.dma_start(x1_sb[i][:, :, :], x1_blocks[bass.ds(n + 2, 1), :, :, :].rearrange("o p j c -> (o p) j c")).then_inc(x1_loaded[i], 16)
            for i in range(2):
                for j in range(J):
                    store(blocks - 2 + i, j)
                if i == 0:
                    sp.dma_start(x1_sb[0][:, :, :], x1_blocks[0, :, :, :]).then_inc(x1_loaded[0], 16)
            sp.wait_ge(x1_loaded[0], 16 * (blocks // 2) + 16)
            for j in range(J):
                sp.wait_ge(stored[j], 16 * (blocks + (j >= 2)))

        @block.tensor
        def _(pe):
            def transposes(n):
                for k in range(KB):
                    if k < 2:
                        pe.wait_ge(xn_ready, n + 1)
                        if not isinstance(n, int):
                            pe.wait_ge(xT_ready[k + 2], n)
                    else:
                        pe.wait_ge(xT_ready[k - 2], n + 1)
                    for j in range(J):
                        last = nc.tensor.transpose(xT_ps[k % 2][:, j * P:(j + 1) * P], xn[:, j, k * P:(k + 1) * P], eye_sb[:])
                    last.then_inc(xT_in_psum[k], 1)

            def step(n):
                for m in range(KB):
                    pe.wait_ge(relu_done[(m + 2) % 4], n + 1)
                    for k in range(KB):
                        if m == 0:
                            pe.wait_ge(m_ready[1][k], n + 1)
                        last = split3(k_ps[m % 2][:], w_hi[WK][:, k, m * P:(m + 1) * P], w_lo[WK][:, k, m * P:(m + 1) * P],
                                      m_hi[1][:, k, :], m_lo[1][:, k, :], k == 0, k == KB - 1)
                    last.then_inc(k_in_psum[m], 1)
                for j in range(J):
                    tok = slice(j * P, (j + 1) * P)
                    pe.wait_ge(gate_ready[(j + 2) % 4], n + 1)
                    for k in range(KB):
                        if j == 0:
                            pe.wait_ge(m_ready[0][k], n + 1)
                        last = split3(r_ps[j % 2][:], m_hi[0][:, k, tok], m_lo[0][:, k, tok],
                                      w_hi[WR][:, k, :], w_lo[WR][:, k, :], k == 0, k == KB - 1)
                    last.then_inc(r_in_psum[j], 1)
                transposes(n + 1)
                for j in range(J):
                    tok = slice(j * P, (j + 1) * P)
                    pe.wait_ge(gated_ready[(j + 2) % 4], n + 1 + (j >= 2))
                    for k in range(KB):
                        if j == 0:
                            pe.wait_ge(ka_ready[k], n + 1 + (k >= 2))
                        last = split3(v_ps[j % 2][:], ka_hi[:, k, tok], ka_lo[:, k, tok],
                                      w_hi[WV][:, k, :], w_lo[WV][:, k, :], k == 0, k == KB - 1)
                    last.then_inc(v_in_psum[j], 1)

            for i in (2, 3):
                pe.sem_inc(relu_done[i], 1)
                pe.sem_inc(gate_ready[i], 1)
            pe.wait_ge(consts_loaded, 32)
            transposes(0)
            pe.wait_ge(w_lo_ready, 3)
            with pe.Fori(0, B) as b:
                for i in range(N):
                    step(b * N + i)

        @block.scalar
        def _(act):
            def part_of_previous(m, k, count):
                act.wait_ge(xT_ready[k], count)
                nc.scalar.activation(part[m][k % 2][:], xT[:, k, 0:T], ACT.Copy,
                                     scale=rest_sb[:, m, k:k + 1]).then_inc(part_ready[m], 1)

            def mixed_high(m, k, count):
                act.wait_ge(mixed_ready[m], count * KB - (KB - 1 - k))
                nc.scalar.copy(m_hi[m][:, k, :], mixed[m][k % 2][:]).then_inc(m_hi_ready[m], 1)

            def gather_xT(count):
                for k in range(KB):
                    act.wait_ge(xT_in_psum[k], count)
                    act.wait_ge(carried, count)
                    nc.scalar.copy(xT[:, k, 1:T + 1], xT_ps[k % 2][:]).then_inc(xT_ready[k], 1)

            def mix_keys(count):
                part_of_previous(1, 0, count)
                for k in range(KB):
                    if k + 1 < KB:
                        part_of_previous(1, k + 1, count)
                    mixed_high(1, k, count)

            def step(n):
                part_of_previous(0, 0, n + 1)
                for k in range(KB):
                    if k + 1 < KB:
                        part_of_previous(0, k + 1, n + 1)
                    mixed_high(0, k, n + 1)
                    act.wait_ge(k_in_psum[k], n + 1)
                    nc.scalar.activation(k_relu[k % 2][:], k_ps[k % 2][:], ACT.Relu).then_inc(relu_done[k], 1)
                    if k >= 1:
                        act.wait_ge(square_done[k - 1], n + 1)
                        nc.scalar.copy(ka_hi[:, k - 1, :], k_square[(k - 1) % 2][:]).then_inc(ka_hi_ready[k - 1], 1)
                act.wait_ge(square_done[KB - 1], n + 1)
                nc.scalar.copy(ka_hi[:, KB - 1, :], k_square[(KB - 1) % 2][:]).then_inc(ka_hi_ready[KB - 1], 1)
                for j in range(J):
                    act.wait_ge(r_in_psum[j], n + 1)
                    act.wait_ge(gated_ready[j], n + 1)
                    nc.scalar.activation(gate[:, j, :], r_ps[j % 2][:], ACT.Sigmoid).then_inc(gate_ready[j], 1)
                gather_xT(n + 2)
                mix_keys(n + 2)

            gather_xT(1)
            act.wait_ge(rest_ready, 1)
            for i in (WK, WR, WV):
                nc.scalar.copy(w_hi[i][:, :, :], w_raw[i][:, :, :]).then_inc(w_hi_ready, 1)
            mix_keys(1)
            with act.Fori(0, B) as b:
                for i in range(N):
                    step(b * N + i)

        @block.vector
        def _(dve):
            def statistics(slot, loads):
                dve.wait_ge(x1_loaded[slot], loads)
                for j in range(J):
                    last = nc.vector.bn_stats(stats[:, j, :], x1_sb[slot][:, j, :])
                last.then_inc(stats_done, 1)

            def mean_and_variance():
                for j in range(J):
                    last = nc.vector.bn_aggr(mean_var[:, j, :], stats[:, j, :])
                last.then_inc(meanvar_ready, 1)

            def normalize(slot, count):
                dve.wait_ge(rstd_ready, count)
                for j in range(J):
                    last = nc.vector.tensor_scalar(xn[:, j, :], x1_sb[slot][:, j, :], mean_var[:, j, 0:1],
                                                   rstd[:, 3, j:j + 1], ALU.subtract, ALU.mult)
                last.then_inc(xn_ready, 1)

            def mix(m, k, count):
                dve.wait_ge(part_ready[m], count * KB - (KB - 1 - k))
                if k >= 2:
                    dve.wait_ge(m_ready[m][k - 2], count)
                nc.vector.scalar_tensor_tensor(mixed[m][k % 2][:], xT[:, k, 1:T + 1], mu_sb[:, m, k:k + 1],
                                               part[m][k % 2][:], ALU.mult, ALU.add).then_inc(mixed_ready[m], 1)

            def mixed_low(m, k, count):
                dve.wait_ge(m_hi_ready[m], count * KB - (KB - 1 - k))
                nc.vector.tensor_tensor(m_lo[m][:, k, :], mixed[m][k % 2][:], m_hi[m][:, k, :].bitcast(F32),
                                        ALU.subtract).then_inc(m_ready[m][k], 1)

            def activation_low(k, count):
                dve.wait_ge(ka_hi_ready[k], count)
                nc.vector.tensor_tensor(ka_lo[:, k, :], k_square[k % 2][:], ka_hi[:, k, :].bitcast(F32),
                                        ALU.subtract).then_inc(ka_ready[k], 1)

            def apply_gate(j, n):
                dve.wait_ge(v_in_psum[j], n + 1)
                dve.wait_ge(gate_ready[j], n + 1 + (j >= 2))
                dve.wait_ge(result_ready[(j + 2) % 4], n + 1)
                nc.vector.tensor_tensor(gated[j % 2][:], v_ps[j % 2][:], gate[:, j, :], ALU.mult).then_inc(gated_ready[j], 1)

            def step(n, i, loads):
                mix(0, 0, n + 1)
                for k in range(KB):
                    if k + 1 < KB:
                        mix(0, k + 1, n + 1)
                    mixed_low(0, k, n + 1)
                    if k >= 1:
                        activation_low(k - 1, n + 1)
                activation_low(KB - 1, n + 1)
                slot = (i + 1) % 2
                statistics(slot, loads)
                dve.wait_ge(stats_done, n + 2)
                if i + 1 < N:
                    nc.vector.tensor_copy(xT[:, :, 0:1], xT[:, :, T:T + 1]).then_inc(carried, 1)
                else:
                    nc.vector.memset(xT[:, :, 0:1], 0.0).then_inc(carried, 1)
                mean_and_variance()
                normalize(slot, n + 2)
                mix(1, 0, n + 2)
                mix(1, 1, n + 2)
                mixed_low(1, 0, n + 2)
                apply_gate(0, n)
                mix(1, 2, n + 2)
                mixed_low(1, 1, n + 2)
                apply_gate(1, n)
                mix(1, 3, n + 2)
                mixed_low(1, 2, n + 2)
                mixed_low(1, 3, n + 2)
                apply_gate(2, n)
                apply_gate(3, n)

            for j in range(J):
                dve.sem_inc(gated_ready[j], 1)
            nc.vector.memset(xT[:, :, 0:1], 0.0).then_inc(carried, 1)
            nc.vector.memset(epsilon[:], LN_EPS)
            nc.vector.memset(three_halves[:], 1.5)
            nc.vector.memset(power[:], -0.5).then_inc(consts_set, 1)
            statistics(0, 16)
            dve.wait_ge(stats_done, 1)
            mean_and_variance()
            normalize(0, 1)
            dve.wait_ge(consts_loaded, 32)
            nc.vector.tensor_scalar(rest_sb[:, :, :], mu_sb[:, :, :], -1.0, 1.0, ALU.mult, ALU.add).then_inc(rest_ready, 1)
            for count, w in enumerate((WK, WR, WV)):
                dve.wait_ge(w_hi_ready, count + 1)
                nc.vector.tensor_tensor(w_lo[w][:, :, :], w_raw[w][:, :, :], w_hi[w][:, :, :].bitcast(F32),
                                        ALU.subtract).then_inc(w_lo_ready, 1)
            mix(1, 0, 1)
            for k in range(KB):
                if k + 1 < KB:
                    mix(1, k + 1, 1)
                mixed_low(1, k, 1)
            with dve.Fori(0, B) as b:
                for i in range(N):
                    step(b * N + i, i, (b * (N // 2) + (i + 1) // 2) * 16 + 16)

        @block.gpsimd
        def _(pool):
            def inverse_deviation(count):
                var, y, t, out_y = (rstd[:, i, :] for i in range(4))
                pool.wait_ge(meanvar_ready, count)
                nc.gpsimd.tensor_tensor(var, mean_var[:, :, 1], epsilon[:], ALU.add).then_inc(rstd_step, 1)
                pool.wait_ge(rstd_step, 6 * count - 5)
                nc.gpsimd.tensor_tensor(y, var, power[:], ALU.pow).then_inc(rstd_step, 1)
                pool.wait_ge(rstd_step, 6 * count - 4)
                nc.gpsimd.tensor_tensor(t, y, y, ALU.mult).then_inc(rstd_step, 1)
                pool.wait_ge(rstd_step, 6 * count - 3)
                nc.gpsimd.tensor_tensor(t, t, var, ALU.mult).then_inc(rstd_step, 1)
                pool.wait_ge(rstd_step, 6 * count - 2)
                nc.gpsimd.tensor_tensor(t, t, power[:], ALU.mult).then_inc(rstd_step, 1)
                pool.wait_ge(rstd_step, 6 * count - 1)
                nc.gpsimd.tensor_tensor(t, t, three_halves[:], ALU.add).then_inc(rstd_step, 1)
                pool.wait_ge(rstd_step, 6 * count)
                nc.gpsimd.tensor_tensor(out_y, t, y, ALU.mult).then_inc(rstd_ready, 1)

            def step(n, i):
                for m in range(KB):
                    pool.wait_ge(relu_done[m], n + 1 + (m >= 2))
                    pool.wait_ge(ka_ready[(m + 2) % 4], n + 1)
                    nc.gpsimd.tensor_tensor(k_square[m % 2][:], k_relu[m % 2][:], k_relu[m % 2][:], ALU.mult).then_inc(square_done[m], 1)
                inverse_deviation(n + 2)
                for j in range(J):
                    pool.wait_ge(gated_ready[j], n + 2)
                    pool.wait_ge(stored[(j + 2) % 4], n * 16 + 16)
                    nc.gpsimd.tensor_tensor(result[j % 2][:], gated[j % 2][:], x1_sb[i % 2][:, j, :], ALU.add).then_inc(result_ready[j], 1)

            for i in (2, 3):
                pool.sem_inc(ka_ready[i], 1)
                pool.sem_inc(result_ready[i], 1)
                pool.sem_inc(stored[i], 16)
            pool.wait_ge(consts_set, 1)
            inverse_deviation(1)
            with pool.Fori(0, B) as b:
                for i in range(N):
                    step(b * N + i, i)


def layer(nc, x, wq, wk, wv, wo, w_r, w_k, w_v, mu, tables, mask, tri, eye, out):
    B, L, _ = x.shape
    x1_dram = nc.dram_tensor("x1_dram", [B * L, C], F32, kind="Internal").ap()
    with ExitStack() as ctx:
        def sem(name):
            return ctx.enter_context(nc.semaphore(name))

        ffn_raw = [ctx.enter_context(nc.sbuf_tensor(f"ffn_raw{i}", [P, KB, C], F32)) for i in range(3)]
        attention_phase(nc, sem, x, wq, wk, wv, wo, tables, mask, tri, eye, x1_dram, ffn_raw, [w_r, w_k, w_v])
        mix_phase(nc, sem, x1_dram, ffn_raw, mu, eye, out, L // 512)


def constants(length):
    theta = np.float32(10000.0)
    inv_freq = np.float32(1.0) / np.power(theta, np.arange(0, D, 2, dtype=np.float32) / np.float32(D), dtype=np.float32)
    angle = np.arange(length, dtype=np.float32)[:, None] * inv_freq[None, :]
    cos, sin = np.cos(angle), np.sin(angle)
    row = np.concatenate([np.repeat(cos, 2, axis=1), np.stack([-sin, sin], axis=-1).reshape(length, D)], axis=1)
    table = row.reshape(length // P, P, 2 * D).transpose(1, 0, 2)
    table = np.ascontiguousarray(np.concatenate([table, table[:, :1]], axis=1))
    at = np.arange(P)
    upto = (at[:, None] <= at[None, :]).astype(np.float32)
    after = np.float32(1.0) - upto
    return {"tables": table, "mask": upto, "tri": np.concatenate([upto, after], axis=1),
            "eye": np.eye(P, dtype=np.float32)}


def kernel(L0_attn_x, L0_attn_wq, L0_attn_wk, L0_attn_wv, L0_attn_wo, L0_ffn_W_r, L0_ffn_W_k, L0_ffn_W_v,
           L0_ffn_mu_r, L0_ffn_mu_k):
    import concourse.bacc as bacc
    from concourse.bass_utils import run_bass_kernel_spmd

    x = np.asarray(L0_attn_x)
    arrays = {
        "x": x, "wq": np.asarray(L0_attn_wq), "wk": np.asarray(L0_attn_wk), "wv": np.asarray(L0_attn_wv),
        "wo": np.asarray(L0_attn_wo),
        "w_r": np.asarray(L0_ffn_W_r).T, "w_k": np.asarray(L0_ffn_W_k).T, "w_v": np.asarray(L0_ffn_W_v).T,
        "mu": np.stack([np.asarray(L0_ffn_mu_r), np.asarray(L0_ffn_mu_k)]).reshape(2, KB, P).transpose(2, 0, 1),
        **constants(x.shape[1]),
    }
    arrays = {name: np.ascontiguousarray(a) for name, a in arrays.items()}
    nc = bacc.Bacc("TRN2", target_bir_lowering=False, num_devices=1)
    ins = {name: nc.dram_tensor(f"in_{name}", a.shape, F32, kind="ExternalInput").ap() for name, a in arrays.items()}
    out = nc.dram_tensor("out", x.shape, F32, kind="ExternalOutput").ap()
    layer(nc, out=out, **ins)
    got = run_bass_kernel_spmd(nc, [{f"in_{name}": a for name, a in arrays.items()}], core_ids=[0])
    return got.results[0]["out"]
```

```python
from contextlib import ExitStack

import numpy as np

import concourse.bass as bass
from concourse import mybir

F32 = mybir.dt.float32
F32R = mybir.dt.float32r
ALU = mybir.AluOpType
ACT = mybir.ActivationFunctionType
AX_X = mybir.AxisListType.X

P = 128
C = 512
KB = C // P
H = 16
D = C // H
HG = P // D
G = H // HG
UNROLL = 4
T = 512
J = T // P
LN_EPS = 1e-5
DEN_EPS = 1e-6


class BlockNorm:

    def __init__(self, ctx, nc, sem):
        def sb(name, shape):
            return ctx.enter_context(nc.sbuf_tensor(name, shape, F32))

        self.nc = nc
        self.eye = sb("eye_sb", [P, P])
        self.power, self.epsilon, self.three_halves = sb("power", [P, J]), sb("epsilon", [P, J]), sb("three_halves", [P, J])
        self.x1 = [sb(f"x1_sb{i}", [P, J, C]) for i in range(2)]
        self.stats, self.mean_var = sb("f_stats", [P, J, 6]), sb("f_mean_var", [P, J, 2])
        self.rstd, self.xn = sb("f_rstd", [P, 4, J]), sb("f_xn", [P, J, C])
        self.x1_loaded = [sem(f"x1_loaded{i}") for i in range(2)]
        self.stats_done, self.meanvar_ready = sem("f_stats_done"), sem("f_meanvar_ready")
        self.rstd_step, self.rstd_ready, self.xn_ready = sem("f_rstd_step"), sem("f_rstd_ready"), sem("f_xn_ready")

    def statistics(self, dve, slot, loads):
        dve.wait_ge(self.x1_loaded[slot], loads)
        for j in range(J):
            last = self.nc.vector.bn_stats(self.stats[:, j, :], self.x1[slot][:, j, :])
        last.then_inc(self.stats_done, 1)

    def mean_and_variance(self):
        for j in range(J):
            last = self.nc.vector.bn_aggr(self.mean_var[:, j, :], self.stats[:, j, :])
        last.then_inc(self.meanvar_ready, 1)

    def normalize(self, dve, slot, count):
        dve.wait_ge(self.rstd_ready, count)
        for j in range(J):
            last = self.nc.vector.tensor_scalar(self.xn[:, j, :], self.x1[slot][:, j, :], self.mean_var[:, j, 0:1],
                                                self.rstd[:, 3, j:j + 1], ALU.subtract, ALU.mult)
        last.then_inc(self.xn_ready, 1)

    def inverse_deviation(self, pool, count):
        pool.wait_ge(self.meanvar_ready, count)
        inverse_square_root(self.nc, pool, self.mean_var[:, :, 1], [self.rstd[:, i, :] for i in range(4)],
                            self.power[:], self.epsilon[:], self.three_halves[:], self.rstd_step, self.rstd_ready, count)


def inverse_square_root(nc, pool, variance, columns, power, epsilon, three_halves, step, done, count):
    var, y, t, result = columns
    nc.gpsimd.tensor_tensor(var, variance, epsilon, ALU.add).then_inc(step, 1)
    pool.wait_ge(step, 6 * count - 5)
    nc.gpsimd.tensor_tensor(y, var, power, ALU.pow).then_inc(step, 1)
    pool.wait_ge(step, 6 * count - 4)
    nc.gpsimd.tensor_tensor(t, y, y, ALU.mult).then_inc(step, 1)
    pool.wait_ge(step, 6 * count - 3)
    nc.gpsimd.tensor_tensor(t, t, var, ALU.mult).then_inc(step, 1)
    pool.wait_ge(step, 6 * count - 2)
    nc.gpsimd.tensor_tensor(t, t, power, ALU.mult).then_inc(step, 1)
    pool.wait_ge(step, 6 * count - 1)
    nc.gpsimd.tensor_tensor(t, t, three_halves, ALU.add).then_inc(step, 1)
    pool.wait_ge(step, 6 * count)
    nc.gpsimd.tensor_tensor(result, t, y, ALU.mult).then_inc(done, 1)


def attention_phase(nc, sem, norm, x, wq, wk, wv, wo, tables, mask, tri, eye, x1_dram, ffn_raw, ffn_w):
    B, L, _ = x.shape
    tiles = B * L // P
    per_batch = L // P
    inner = per_batch // UNROLL
    x_tiles = x.rearrange("b (n p) c -> (b n) p c", p=P)
    x1_tiles = x1_dram.rearrange("(n p) c -> n p c", p=P)
    x1_blocks = x1_dram.rearrange("(n j p) c -> n p j c", p=P, j=J)
    eye_sb = norm.eye

    with ExitStack() as ctx:
        def sb(name, shape, dt=F32):
            return ctx.enter_context(nc.sbuf_tensor(name, shape, dt))

        def bank(name):
            return ctx.enter_context(nc.psum_tensor(name, [P, 512], F32))

        w_dram = [wk, wq, wv, wo]
        w_hi = [sb(f"w_hi{i}", [P, KB, C], F32R) for i in range(4)]
        w_lo = [sb(f"w_lo{i}", [P, KB, C], F32R) for i in range(4)]
        WK, WQ, WV, WO = range(4)
        table_sb = sb("table_sb", [P, per_batch + 1, 2 * D])
        mask_sb = sb("mask_sb", [P, P])
        tri_sb = sb("tri_sb", [P, 2 * P])
        tri_r = sb("tri_r", [P, 2 * P], F32R)
        zeros_r = sb("zeros_r", [P, C], F32R)
        x_sb = [sb(f"x_sb{u}", [P, C]) for u in range(UNROLL)]
        stats = [sb(f"stats{u}", [P, 6]) for u in range(2)]
        mean_var = [sb(f"mean_var{u}", [P, 2]) for u in range(2)]
        rstd = [sb(f"rstd{u}", [P, 4]) for u in range(2)]
        xn = sb("xn", [P, C])
        xnT_hi = [sb(f"xnT_hi{u}", [P, KB, P], F32R) for u in range(2)]
        xnT_lo = [sb(f"xnT_lo{u}", [P, KB, P], F32R) for u in range(2)]
        k_cos, k_sin, k_sum = sb("k_cos", [P, C]), sb("k_sin", [P, C]), sb("k_sum", [P, C])
        q_cos, q_sin, q_sum = sb("q_cos", [P, C]), sb("q_sin", [P, C]), sb("q_sum", [P, C])
        k_nat = [sb(f"k_nat{u}", [P, C]) for u in range(2)]
        k_hi, k_lo = sb("k_hi", [P, C], F32R), sb("k_lo", [P, C], F32R)
        q_nat, q_norm, v_nat = sb("q_nat", [P, C]), sb("q_norm", [P, C]), sb("v_nat", [P, C])
        prod = sb("prod", [P, C])
        den = sb("den", [P, 3, H])
        kT_hi, kT_lo = sb("kT_hi", [P, G, P], F32R), sb("kT_lo", [P, G, P], F32R)
        qT = sb("qT", [P, G, P])
        qx_hi, qx_lo = sb("qx_hi", [P, G, HG, P], F32R), sb("qx_lo", [P, G, HG, P], F32R)
        probs = sb("probs", [P, G, HG * P])
        state = sb("state", [P, G, P])
        oT_hi, oT_lo = sb("oT_hi", [P, G, P], F32R), sb("oT_lo", [P, G, P], F32R)

        bank0, bank1, bank2, bank3 = bank("bank0"), bank("bank1"), bank("bank2"), bank("bank3")
        bank4, bank5, kcum, kv = bank("bank4"), bank("bank5"), bank("kcum"), bank("kv")
        xnT_ps, outT_ps = bank0, bank0
        attn_ps = bank1
        kT_ps, qT_ps = bank2, bank5
        k_ps, v_ps, q_ps = bank3, bank3, bank4
        score_ps = [bank0, bank1, bank2, bank5]

        consts_loaded, table_loaded, ffn_loaded = sem("consts_loaded"), sem("table_loaded"), sem("ffn_loaded")
        w_loaded = [sem(f"w_loaded{i}") for i in range(4)]
        w_hi_ready, w_lo_ready = sem("w_hi_ready"), sem("w_lo_ready")
        tri_ready, consts_set, zeros_set = sem("tri_ready"), sem("consts_set"), sem("zeros_set")
        x_loaded = [sem(f"x_loaded{u}") for u in range(UNROLL)]
        x1_stored = [sem(f"x1_stored{u}") for u in range(UNROLL)]
        stats_done, meanvar_ready, rstd_ready = sem("stats_done"), sem("meanvar_ready"), sem("rstd_ready")
        rstd_step = sem("rstd_step")
        xn_ready = sem("xn_ready")
        xnT_in_psum, xnT_hi_ready, xnT_ready = sem("xnT_in_psum"), sem("xnT_hi_ready"), sem("xnT_ready")
        k_in_psum, q_in_psum, v_in_psum = sem("k_in_psum"), sem("q_in_psum"), sem("v_in_psum")
        k_rotated, q_rotated = sem("k_rotated"), sem("q_rotated")
        k_summed, q_summed = sem("k_summed"), sem("q_summed")
        k_ready, k_hi_ready, k_split, k_split_used = sem("k_ready"), sem("k_hi_ready"), sem("k_split"), sem("k_split_used")
        q_ready, v_ready = sem("q_ready"), sem("v_ready")
        kcum_ready, kcum_used = sem("kcum_ready"), sem("kcum_used")
        den_summed, den_guarded, den_inverted, q_normed = sem("den_summed"), sem("den_guarded"), sem("den_inverted"), sem("q_normed")
        kT_in_psum, kT_hi_ready, kT_ready = sem("kT_in_psum"), sem("kT_hi_ready"), sem("kT_ready")
        qT_in_psum, qx_ready = sem("qT_in_psum"), sem("qx_ready")
        qx_hi_ready = [sem(f"qx_hi_ready{q}") for q in range(HG)]
        kv_ready, state_ready = sem("kv_ready"), sem("state_ready")
        scores_ready = [sem(f"scores_ready{g}") for g in range(G)]
        scores_free = [sem(f"scores_free{g}") for g in range(G)]
        outT_in_psum, oT_hi_ready, oT_ready = sem("outT_in_psum"), sem("oT_hi_ready"), sem("oT_ready")
        attn_ready, x1_ready = sem("attn_ready"), sem("x1_ready")

        block = ctx.enter_context(nc.Block())

        def heads(ap):
            return ap.rearrange("p (h d) -> p h d", d=D)

        raw = [ffn_raw[0][:, :, :], ffn_raw[1][:, :, :], ffn_raw[2][:, :, :], probs[:, :, :]]

        def split3(psum, lhs_hi, lhs_lo, rhs_hi, rhs_lo, start, stop):
            nc.tensor.matmul(psum, lhs_hi, rhs_hi, start=start, stop=False)
            nc.tensor.matmul(psum, lhs_lo, rhs_hi, start=False, stop=False)
            return nc.tensor.matmul(psum, lhs_hi, rhs_lo, start=False, stop=stop)

        @block.sync
        def _(sp):
            for u in range(2):
                sp.dma_start(x_sb[u][:], x_tiles[u, :, :]).then_inc(x_loaded[u], 16)
            sp.dma_start(raw[WK], w_dram[WK].rearrange("(k p) n -> p k n", p=P)).then_inc(w_loaded[WK], 16)
            for dst, src in ((eye_sb, eye), (tri_sb, tri), (mask_sb, mask)):
                sp.dma_start(dst[:], src).then_inc(consts_loaded, 16)
            for i in (WQ,):
                sp.dma_start(raw[i], w_dram[i].rearrange("(k p) n -> p k n", p=P)).then_inc(w_loaded[i], 16)
            sp.dma_start(table_sb[:, :, :], tables).then_inc(table_loaded, 16)
            for u in range(2, UNROLL):
                sp.dma_start(x_sb[u][:], x_tiles[u, :, :]).then_inc(x_loaded[u], 16)
            for i in (WV, WO):
                sp.dma_start(raw[i], w_dram[i].rearrange("(k p) n -> p k n", p=P)).then_inc(w_loaded[i], 16)
            sp.wait_ge(w_lo_ready, 3)
            for i in range(3):
                sp.dma_start(ffn_raw[i][:, :, :], ffn_w[i].rearrange("(k p) n -> p k n", p=P)).then_inc(ffn_loaded, 16)

            def store(tile, turn, u):
                sp.wait_ge(x1_ready, tile + 2)
                sp.dma_start(x1_tiles[bass.ds(tile, 1), :, :].rearrange("o p c -> (o p) c"),
                             x_sb[u][:]).then_inc(x1_stored[u], 16)
                sp.wait_ge(x1_stored[u], 16 * turn + 16)

            def turns(first, last):
                with sp.Fori(first, last) as turn:
                    for u in range(UNROLL):
                        tile = turn * UNROLL + u
                        store(tile, turn, u)
                        sp.dma_start(x_sb[u][:], x_tiles[bass.ds(tile + UNROLL, 1), :, :].rearrange("o p c -> (o p) c")).then_inc(x_loaded[u], 16)

            turns(0, inner)
            for i in range(2):
                sp.dma_start(norm.x1[i][:, :, :], x1_blocks[i, :, :, :]).then_inc(norm.x1_loaded[i], 16)
            turns(inner, tiles // UNROLL - 1)
            for u in range(UNROLL):
                store(tiles - UNROLL + u, tiles // UNROLL - 1, u)
                if u < 2:
                    sp.dma_start(x_sb[u][:], x_tiles[u, :, :]).then_inc(x_loaded[u], 16)
            for u in range(2):
                sp.wait_ge(x_loaded[u], 16 * (tiles // UNROLL) + 16)
            sp.wait_ge(ffn_loaded, 48)

        @block.tensor
        def _(pe):
            def transpose_xn():
                for k in range(KB):
                    last = nc.tensor.transpose(xnT_ps[:, k * P:(k + 1) * P], xn[:, k * P:(k + 1) * P], eye_sb[:])
                last.then_inc(xnT_in_psum, 1)

            def project(psum, slot, w, blocks=range(KB)):
                for k in blocks:
                    last = split3(psum[:], xnT_hi[slot][:, k, :], xnT_lo[slot][:, k, :],
                                  w_hi[w][:, k, :], w_lo[w][:, k, :], k == 0, k == KB - 1)
                return last

            def step(tile, u):
                ahead, here = (u + 1) % 2, u % 2
                pe.wait_ge(k_ready, tile + 1)
                pe.wait_ge(scores_free[2], tile + 1)
                for g in range(G):
                    last = nc.tensor.transpose(kT_ps[:, g * P:(g + 1) * P], k_nat[here][:, g * P:(g + 1) * P], eye_sb[:])
                last.then_inc(kT_in_psum, 1)
                pe.wait_ge(k_split, tile + 1)
                nc.tensor.matmul(kcum[:], tri_r[:, 0:P], k_hi[:], start=False, stop=False, skip_group_check=True)
                nc.tensor.matmul(kcum[:], tri_r[:, 0:P], k_lo[:], start=False, stop=True,
                                 skip_group_check=True).then_inc(kcum_ready, 1)
                pe.wait_ge(xnT_ready, tile + 2)
                pe.wait_ge(v_ready, tile + 1)
                project(k_ps, ahead, WK).then_inc(k_in_psum, 1)
                pe.wait_ge(kcum_used, tile + 1)
                nc.tensor.matmul(kcum[:], tri_r[:, P:2 * P], k_hi[:], start=False, stop=False, skip_group_check=True)
                nc.tensor.matmul(kcum[:], tri_r[:, P:2 * P], k_lo[:], start=False, stop=True,
                                 skip_group_check=True).then_inc(k_split_used, 1)
                pe.wait_ge(q_normed, tile + 1)
                pe.wait_ge(scores_free[3], tile + 1)
                for g in range(G):
                    last = nc.tensor.transpose(qT_ps[:, g * P:(g + 1) * P], q_norm[:, g * P:(g + 1) * P], eye_sb[:])
                last.then_inc(qT_in_psum, 1)
                pe.wait_ge(q_rotated, tile + 1)
                project(q_ps, ahead, WQ).then_inc(q_in_psum, 1)
                pe.wait_ge(k_rotated, tile + 2)
                project(v_ps, ahead, WV, range(KB // 2))
                pe.wait_ge(state_ready, tile + 1)
                for g in range(G):
                    for h in range(HG):
                        f = g * P + h * D
                        last = nc.tensor.matmul(kv[h * D:(h + 1) * D, g * D:(g + 1) * D], k_nat[here][:, f:f + D],
                                                v_nat[:, f:f + D], start=False, stop=True, skip_group_check=True)
                last.then_inc(kv_ready, 1)
                pe.wait_ge(kT_ready, tile + 1)
                pe.wait_ge(qx_ready, tile + 1)
                pe.wait_ge(x1_ready, tile + 1)
                for g in range(G):
                    split3(score_ps[g][:], kT_hi[:, g, :], kT_lo[:, g, :],
                           qx_hi[:, g, :, :].rearrange("p a b -> p (a b)"),
                           qx_lo[:, g, :, :].rearrange("p a b -> p (a b)"), True, True).then_inc(scores_ready[g], 1)
                pe.wait_ge(scores_free[0], tile + 2)
                for g in range(G):
                    nc.tensor.matmul(outT_ps[:, g * P:(g + 1) * P], state[:, g, :], qT[:, g, :],
                                     start=(g == 0), stop=False, skip_group_check=True)
                for g in range(G):
                    pe.wait_ge(scores_free[g], tile + 2)
                    for h in range(HG):
                        f = g * P + h * D
                        last = nc.tensor.matmul(outT_ps[h * D:(h + 1) * D, g * P:(g + 1) * P], v_nat[:, f:f + D],
                                                probs[:, g, h * P:(h + 1) * P], start=False,
                                                stop=(g == G - 1 and h == HG - 1), skip_group_check=True)
                last.then_inc(outT_in_psum, 1)
                project(v_ps, ahead, WV, range(KB // 2, KB)).then_inc(v_in_psum, 1)
                pe.wait_ge(xn_ready, tile + 3)
                pe.wait_ge(oT_ready, tile + 2)
                transpose_xn()
                for g in range(G):
                    last = split3(attn_ps[:], oT_hi[:, g, :], oT_lo[:, g, :], w_hi[WO][:, g, :], w_lo[WO][:, g, :],
                                  g == 0, g == G - 1)
                last.then_inc(attn_ready, 1)

            pe.wait_ge(consts_loaded, 48)
            pe.wait_ge(consts_set, 1)
            pe.wait_ge(xn_ready, 1)
            transpose_xn()
            pe.wait_ge(xnT_ready, 1)
            pe.wait_ge(w_lo_ready, 1)
            project(k_ps, 0, WK).then_inc(k_in_psum, 1)
            pe.wait_ge(w_lo_ready, 2)
            project(q_ps, 0, WQ).then_inc(q_in_psum, 1)
            pe.wait_ge(w_lo_ready, 3)
            pe.wait_ge(k_rotated, 1)
            project(v_ps, 0, WV).then_inc(v_in_psum, 1)
            pe.wait_ge(xn_ready, 2)
            transpose_xn()
            pe.wait_ge(w_lo_ready, 4)
            pe.wait_ge(tri_ready, 1)
            with pe.Fori(0, B) as b:
                nc.tensor.matmul(kcum[:], zeros_r[:, 0:P], zeros_r[:], start=True, stop=True, skip_group_check=True)
                nc.tensor.matmul(kv[:], zeros_r[:, 0:P], zeros_r[:], start=True, stop=True,
                                 skip_group_check=True).then_inc(kv_ready, 1)
                with pe.Fori(0, inner) as turn:
                    for u in range(UNROLL):
                        step(b * per_batch + turn * UNROLL + u, u)

        @block.scalar
        def _(act):
            def xnT_high(slot, count):
                act.wait_ge(xnT_in_psum, count)
                nc.scalar.copy(xnT_hi[slot][:, :, :].rearrange("p k n -> p (k n)"), xnT_ps[:]).then_inc(xnT_hi_ready, 1)

            def keys(slot, count):
                act.wait_ge(k_summed, count)
                nc.scalar.activation(k_nat[slot][:], k_sum[:], ACT.Relu).then_inc(k_ready, 1)
                act.wait_ge(k_ready, count)
                nc.scalar.copy(k_hi[:], k_nat[slot][:]).then_inc(k_hi_ready, 1)

            def queries(count):
                act.wait_ge(q_summed, count)
                nc.scalar.activation(q_nat[:], q_sum[:], ACT.Relu).then_inc(q_ready, 1)

            def values(count):
                act.wait_ge(v_in_psum, count)
                nc.scalar.copy(v_nat[:], v_ps[:]).then_inc(v_ready, 1)

            def step(b, tile, u):
                act.wait_ge(kT_in_psum, tile + 1)
                nc.scalar.copy(kT_hi[:, :, :].rearrange("p g n -> p (g n)"), kT_ps[:]).then_inc(kT_hi_ready, 1)
                act.wait_ge(kv_ready, tile + b + 1)
                for q in range(HG):
                    own = slice(q * D, (q + 1) * D)
                    last = nc.scalar.copy(state[own, :, own], kv[own, 0:G * D].rearrange("p (g n) -> p g n", g=G))
                last.then_inc(state_ready, 1)
                act.wait_ge(qT_in_psum, tile + 1)
                nc.scalar.copy(qT[:, :, :].rearrange("p g n -> p (g n)"), qT_ps[:])
                for q in range(HG):
                    own = slice(q * D, (q + 1) * D)
                    nc.scalar.copy(qx_hi[own, :, q, :], qT_ps[own, :].rearrange("p (g n) -> p g n", g=G)).then_inc(qx_hi_ready[q], 1)
                act.wait_ge(k_split_used, tile + 1)
                keys((u + 1) % 2, tile + 2)
                act.wait_ge(q_normed, tile + 1)
                queries(tile + 2)
                act.wait_ge(outT_in_psum, tile + 1)
                nc.scalar.copy(oT_hi[:, :, :].rearrange("p g n -> p (g n)"), outT_ps[:]).then_inc(oT_hi_ready, 1)
                values(tile + 2)
                xnT_high(u % 2, tile + 3)

            for i in (WK, WQ, WV, WO):
                act.wait_ge(w_loaded[i], 16)
                nc.scalar.copy(w_hi[i][:, :, :], raw[i]).then_inc(w_hi_ready, 1)
                if i == WK:
                    xnT_high(0, 1)
            act.wait_ge(consts_loaded, 48)
            nc.scalar.copy(tri_r[:], tri_sb[:]).then_inc(tri_ready, 1)
            keys(0, 1)
            queries(1)
            values(1)
            xnT_high(1, 2)
            act.wait_ge(consts_set, 1)
            act.wait_ge(zeros_set, 1)
            with act.Fori(0, B) as b:
                with act.Fori(0, inner) as turn:
                    for u in range(UNROLL):
                        step(b, b * per_batch + turn * UNROLL + u, u)

        @block.vector
        def _(dve):
            def normalize_stats(slot, loads):
                dve.wait_ge(x_loaded[slot], loads)
                nc.vector.bn_stats(stats[slot % 2][:], x_sb[slot][:]).then_inc(stats_done, 1)

            def mean_and_variance(slot):
                nc.vector.bn_aggr(mean_var[slot % 2][:], stats[slot % 2][:]).then_inc(meanvar_ready, 1)

            def normalize(slot, count):
                dve.wait_ge(rstd_ready, count)
                nc.vector.tensor_scalar(xn[:], x_sb[slot][:], mean_var[slot % 2][:, 0:1], rstd[slot % 2][:, 3:4],
                                        ALU.subtract, ALU.mult).then_inc(xn_ready, 1)

            def xnT_low(slot, count):
                dve.wait_ge(xnT_hi_ready, count)
                nc.vector.tensor_tensor(xnT_lo[slot][:, :, :].rearrange("p k n -> p (k n)"), xnT_ps[:],
                                        xnT_hi[slot][:, :, :].rearrange("p k n -> p (k n)").bitcast(F32),
                                        ALU.subtract).then_inc(xnT_ready, 1)

            def rotate(psum, by_cos, by_sin, position, done):
                pair = table_sb[:, bass.ds(position, 1), :] if not isinstance(position, int) else table_sb[:, position:position + 1, :]
                cos = pair[:, :, 0:D].broadcast_to([P, H, D])
                sin = pair[:, :, D:2 * D].rearrange("p o (f c) -> p o f c", c=2).broadcast_to([P, H, D // 2, 2])
                nc.vector.tensor_tensor(heads(by_cos[:]), heads(psum[:]), cos, ALU.mult)
                swapped = psum[:].rearrange("p (h f c) -> p h f c", h=H, c=2)[:, :, :, ::-1]
                nc.vector.tensor_tensor(by_sin[:].rearrange("p (h f c) -> p h f c", h=H, c=2), swapped, sin,
                                        ALU.mult).then_inc(done, 1)

            def step(turn, tile, all_turn, u):
                dve.wait_ge(q_ready, tile + 1)
                dve.wait_ge(kcum_ready, tile + 1)
                nc.vector.tensor_tensor(prod[:], q_nat[:], kcum[:], ALU.mult).then_inc(kcum_used, 1)
                dve.wait_ge(kcum_used, tile + 1)
                nc.vector.tensor_reduce(den[:, 0, :], heads(prod[:]), AX_X, ALU.add).then_inc(den_summed, 1)
                dve.wait_ge(den_summed, tile + 1)
                nc.vector.tensor_scalar_add(den[:, 1, :], den[:, 0, :], DEN_EPS).then_inc(den_guarded, 1)
                dve.wait_ge(den_guarded, tile + 1)
                nc.vector.reciprocal(den[:, 2, :], den[:, 1, :]).then_inc(den_inverted, 1)
                dve.wait_ge(den_inverted, tile + 1)
                nc.vector.tensor_tensor(heads(q_norm[:]), heads(q_nat[:]),
                                        den[:, 2, :].rearrange("p (h o) -> p h o", o=1).broadcast_to([P, H, D]),
                                        ALU.mult).then_inc(q_normed, 1)
                dve.wait_ge(kT_hi_ready, tile + 1)
                nc.vector.tensor_tensor(kT_lo[:, :, :].rearrange("p g n -> p (g n)"), kT_ps[:],
                                        kT_hi[:, :, :].rearrange("p g n -> p (g n)").bitcast(F32),
                                        ALU.subtract).then_inc(kT_ready, 1)
                dve.wait_ge(k_in_psum, tile + 2)
                dve.wait_ge(k_summed, tile + 1)
                rotate(k_ps, k_cos, k_sin, turn * UNROLL + u + 1, k_rotated)
                ahead = (u + 2) % UNROLL
                normalize_stats(ahead, 16 * all_turn + (16 if u < 2 else 32))
                dve.wait_ge(stats_done, tile + 3)
                for q in range(HG):
                    own = slice(q * D, (q + 1) * D)
                    dve.wait_ge(qx_hi_ready[q], tile + 1)
                    last = nc.vector.tensor_tensor(qx_lo[own, :, q, :], qT_ps[own, :].rearrange("p (g n) -> p g n", g=G),
                                                   qx_hi[own, :, q, :].bitcast(F32), ALU.subtract)
                last.then_inc(qx_ready, 1)
                mean_and_variance(ahead)
                dve.wait_ge(q_in_psum, tile + 2)
                dve.wait_ge(q_summed, tile + 1)
                rotate(q_ps, q_cos, q_sin, turn * UNROLL + u + 1, q_rotated)
                for g in range(G):
                    dve.wait_ge(scores_ready[g], tile + 1)
                    nc.vector.tensor_tensor(probs[:, g, :].rearrange("p (h n) -> p h n", h=HG),
                                            score_ps[g][:].rearrange("p (h n) -> p h n", h=HG),
                                            mask_sb[:].rearrange("p (o n) -> p o n", o=1).broadcast_to([P, HG, P]),
                                            ALU.mult).then_inc(scores_free[g], 1)
                normalize(ahead, tile + 3)
                dve.wait_ge(oT_hi_ready, tile + 1)
                nc.vector.tensor_tensor(oT_lo[:, :, :].rearrange("p g n -> p (g n)"), outT_ps[:],
                                        oT_hi[:, :, :].rearrange("p g n -> p (g n)").bitcast(F32),
                                        ALU.subtract).then_inc(oT_ready, 1)
                xnT_low(u % 2, tile + 3)
                dve.wait_ge(attn_ready, tile + 1)
                nc.vector.tensor_tensor(x_sb[u][:], x_sb[u][:], attn_ps[:], ALU.add).then_inc(x1_ready, 1)

            nc.vector.memset(norm.power[:], -0.5)
            nc.vector.memset(norm.epsilon[:], LN_EPS)
            nc.vector.memset(norm.three_halves[:], 1.5)
            nc.vector.memset(state[:, :, :], 0.0)
            nc.vector.memset(zeros_r[:].bitcast(F32), 0.0).then_inc(consts_set, 1)
            for u in range(2):
                normalize_stats(u, 16)
                dve.wait_ge(stats_done, u + 1)
                mean_and_variance(u)
            normalize(0, 1)
            for free in (oT_ready, x1_ready, *scores_free):
                dve.sem_inc(free, 1)
            for i in (WK, WQ, WV, WO):
                dve.wait_ge(w_hi_ready, i + 1)
                nc.vector.tensor_tensor(w_lo[i][:, :, :], raw[i], w_hi[i][:, :, :].bitcast(F32),
                                        ALU.subtract).then_inc(w_lo_ready, 1)
                if i == WK:
                    xnT_low(0, 1)
                    normalize(1, 2)
                if i == WQ:
                    dve.wait_ge(table_loaded, 16)
                    dve.wait_ge(k_in_psum, 1)
                    rotate(k_ps, k_cos, k_sin, 0, k_rotated)
            dve.wait_ge(q_in_psum, 1)
            rotate(q_ps, q_cos, q_sin, 0, q_rotated)
            xnT_low(1, 2)
            dve.wait_ge(zeros_set, 1)

            def batch(b):
                with dve.Fori(0, inner) as turn:
                    for u in range(UNROLL):
                        step(turn, b * per_batch + turn * UNROLL + u, b * inner + turn + 0, u)

            with dve.Fori(0, B - 1) as b:
                batch(b)
            norm.statistics(dve, 0, 16)
            dve.wait_ge(norm.stats_done, 1)
            norm.mean_and_variance()
            batch(B - 1)
            norm.normalize(dve, 0, 1)

        @block.gpsimd
        def _(pool):
            def inverse_deviation(slot, count):
                pool.wait_ge(meanvar_ready, count)
                inverse_square_root(nc, pool, mean_var[slot][:, 1:2], [rstd[slot][:, i:i + 1] for i in range(4)],
                                    norm.power[:, 0:1], norm.epsilon[:, 0:1], norm.three_halves[:, 0:1],
                                    rstd_step, rstd_ready, count)

            def keys(count):
                pool.wait_ge(k_rotated, count)
                nc.gpsimd.tensor_tensor(k_sum[:], k_cos[:], k_sin[:], ALU.add).then_inc(k_summed, 1)

            def queries(count):
                pool.wait_ge(q_rotated, count)
                nc.gpsimd.tensor_tensor(q_sum[:], q_cos[:], q_sin[:], ALU.add).then_inc(q_summed, 1)

            def keys_low(slot, count):
                pool.wait_ge(k_hi_ready, count)
                nc.gpsimd.tensor_tensor(k_lo[:], k_nat[slot][:], k_hi[:].bitcast(F32), ALU.subtract).then_inc(k_split, 1)

            def step(tile, u):
                pool.wait_ge(k_ready, tile + 1)
                keys(tile + 2)
                inverse_deviation(u % 2, tile + 3)
                pool.wait_ge(q_ready, tile + 1)
                queries(tile + 2)
                keys_low((u + 1) % 2, tile + 2)

            pool.wait_ge(consts_set, 1)
            inverse_deviation(0, 1)
            inverse_deviation(1, 2)
            nc.gpsimd.memset(qx_hi[:, :, :, :].bitcast(F32), 0.0)
            nc.gpsimd.memset(qx_lo[:, :, :, :].bitcast(F32), 0.0).then_inc(zeros_set, 1)
            keys(1)
            queries(1)
            keys_low(0, 1)

            def batch(b):
                with pool.Fori(0, inner) as turn:
                    for u in range(UNROLL):
                        step(b * per_batch + turn * UNROLL + u, u)

            with pool.Fori(0, B - 1) as b:
                batch(b)
            norm.inverse_deviation(pool, 1)
            batch(B - 1)


def mix_phase(nc, sem, norm, x1_dram, w_raw, mu, out, blocks_per_batch):
    N = blocks_per_batch
    blocks = x1_dram.shape[0] // T
    B = blocks // N
    x1_blocks = x1_dram.rearrange("(n j p) c -> n p j c", p=P, j=J)
    out_tiles = out.rearrange("b (n p) c -> (b n) p c", p=P)
    x1_sb, x1_loaded, xn, xn_ready = norm.x1, norm.x1_loaded, norm.xn, norm.xn_ready

    with ExitStack() as ctx:
        def sb(name, shape, dt=F32):
            return ctx.enter_context(nc.sbuf_tensor(name, shape, dt))

        WR, WK, WV = range(3)
        w_hi = [sb(f"f_hi{i}", [P, KB, C], F32R) for i in range(3)]
        w_lo = [sb(f"f_lo{i}", [P, KB, C], F32R) for i in range(3)]
        mu_sb = sb("mu_sb", [P, 2, KB])
        rest_sb = sb("rest_sb", [P, 2, KB])
        xT = sb("xT", [P, KB, T + 1])
        part = [[sb(f"part{m}{i}", [P, T]) for i in range(2)] for m in range(2)]
        mixed = [[sb(f"mixed{m}{i}", [P, T]) for i in range(2)] for m in range(2)]
        m_hi = [sb(f"m_hi{m}", [P, KB, T], F32R) for m in range(2)]
        m_lo = [sb(f"m_lo{m}", [P, KB, T], F32R) for m in range(2)]
        k_relu = [sb(f"k_relu{i}", [P, T]) for i in range(2)]
        k_square = [sb(f"k_square{i}", [P, T]) for i in range(2)]
        ka_hi, ka_lo = sb("ka_hi", [P, KB, T], F32R), sb("ka_lo", [P, KB, T], F32R)
        gate = sb("gate", [P, J, C])
        gated = [sb(f"gated{i}", [P, C]) for i in range(2)]
        result = [sb(f"result{i}", [P, C]) for i in range(2)]

        xT_ps = [ctx.enter_context(nc.psum_tensor(f"xT_ps{i}", [P, 512], F32)) for i in range(2)]
        k_ps = [ctx.enter_context(nc.psum_tensor(f"f_k_ps{i}", [P, 512], F32)) for i in range(2)]
        xT_ps += k_ps
        r_ps = [ctx.enter_context(nc.psum_tensor(f"f_r_ps{i}", [P, 512], F32)) for i in range(2)]
        v_ps = [ctx.enter_context(nc.psum_tensor(f"f_v_ps{i}", [P, 512], F32)) for i in range(2)]

        mu_loaded, rest_ready = sem("mu_loaded"), sem("rest_ready")
        w_hi_ready, w_lo_ready = sem("f_w_hi_ready"), sem("f_w_lo_ready")
        carried = sem("carried")
        def sems(name):
            return [sem(f"{name}{i}") for i in range(4)]
        xT_in_psum, xT_ready = sems("xT_in_psum"), sems("xT_ready")
        part_ready, mixed_ready = [sem("part_r"), sem("part_k")], [sem("mixed_r"), sem("mixed_k")]
        m_hi_ready, m_ready = [sem("m_hi_r"), sem("m_hi_k")], [sems("m_r"), sems("m_k")]
        k_in_psum, relu_done, square_done, ka_hi_ready, ka_ready = sems("f_k_in_psum"), sems("relu_done"), sems("square_done"), sems("ka_hi_ready"), sems("ka_ready")
        r_in_psum, gate_ready, v_in_psum, gated_ready, result_ready = sems("r_in_psum"), sems("gate_ready"), sems("f_v_in_psum"), sems("gated_ready"), sems("result_ready")
        stored = sems("stored")

        block = ctx.enter_context(nc.Block())

        def split3(psum, lhs_hi, lhs_lo, rhs_hi, rhs_lo, start, stop):
            nc.tensor.matmul(psum, lhs_hi, rhs_hi, start=start, stop=False)
            nc.tensor.matmul(psum, lhs_lo, rhs_hi, start=False, stop=False)
            return nc.tensor.matmul(psum, lhs_hi, rhs_lo, start=False, stop=stop)

        @block.sync
        def _(sp):
            sp.dma_start(mu_sb[:, :, :], mu).then_inc(mu_loaded, 16)

            def store(n, j):
                sp.wait_ge(result_ready[j], n + 1 + (j >= 2))
                sp.dma_start(out_tiles[bass.ds(n * J + j, 1), :, :].rearrange("o p c -> (o p) c"), result[j % 2][:]).then_inc(stored[j], 16)

            with sp.Fori(0, blocks // 2 - 1) as pair:
                for i in range(2):
                    n = pair * 2 + i
                    for j in range(J):
                        store(n, j)
                    sp.dma_start(x1_sb[i][:, :, :], x1_blocks[bass.ds(n + 2, 1), :, :, :].rearrange("o p j c -> (o p) j c")).then_inc(x1_loaded[i], 16)
            for i in range(2):
                for j in range(J):
                    store(blocks - 2 + i, j)
                if i == 0:
                    sp.dma_start(x1_sb[0][:, :, :], x1_blocks[0, :, :, :]).then_inc(x1_loaded[0], 16)
            sp.wait_ge(x1_loaded[0], 16 * (blocks // 2) + 16)
            for j in range(J):
                sp.wait_ge(stored[j], 16 * (blocks + (j >= 2)))

        @block.tensor
        def _(pe):
            def transposes(n):
                pe.wait_ge(xn_ready, n + 1)
                for k in range(KB):
                    if k >= 2:
                        pe.wait_ge(relu_done[k], n + 1)
                    for j in range(J):
                        last = nc.tensor.transpose(xT_ps[k][:, j * P:(j + 1) * P], xn[:, j, k * P:(k + 1) * P], norm.eye[:])
                    last.then_inc(xT_in_psum[k], 1)

            def step(n):
                for m in range(KB):
                    pe.wait_ge(relu_done[(m + 2) % 4], n + 1)
                    for k in range(KB):
                        if m == 0:
                            pe.wait_ge(m_ready[1][k], n + 1)
                        last = split3(k_ps[m % 2][:], w_hi[WK][:, k, m * P:(m + 1) * P], w_lo[WK][:, k, m * P:(m + 1) * P],
                                      m_hi[1][:, k, :], m_lo[1][:, k, :], k == 0, k == KB - 1)
                    last.then_inc(k_in_psum[m], 1)
                for j in range(J):
                    tok = slice(j * P, (j + 1) * P)
                    pe.wait_ge(gate_ready[(j + 2) % 4], n + 1)
                    if j == 0:
                        pe.wait_ge(w_lo_ready, 3)
                    for k in range(KB):
                        if j == 0:
                            pe.wait_ge(m_ready[0][k], n + 1)
                        last = split3(r_ps[j % 2][:], m_hi[0][:, k, tok], m_lo[0][:, k, tok],
                                      w_hi[WR][:, k, :], w_lo[WR][:, k, :], k == 0, k == KB - 1)
                    last.then_inc(r_in_psum[j], 1)
                transposes(n + 1)
                for j in range(J):
                    tok = slice(j * P, (j + 1) * P)
                    pe.wait_ge(gated_ready[(j + 2) % 4], n + 1 + (j >= 2))
                    for k in range(KB):
                        if j == 0:
                            pe.wait_ge(ka_ready[k], n + 1 + (k >= 2))
                        last = split3(v_ps[j % 2][:], ka_hi[:, k, tok], ka_lo[:, k, tok],
                                      w_hi[WV][:, k, :], w_lo[WV][:, k, :], k == 0, k == KB - 1)
                    last.then_inc(v_in_psum[j], 1)

            for i in (2, 3):
                pe.sem_inc(relu_done[i], 1)
                pe.sem_inc(gate_ready[i], 1)
            transposes(0)
            pe.wait_ge(w_lo_ready, 1)
            with pe.Fori(0, B) as b:
                for i in range(N):
                    step(b * N + i)

        @block.scalar
        def _(act):
            def part_of_previous(m, k, count):
                act.wait_ge(xT_ready[k], count)
                nc.scalar.activation(part[m][k % 2][:], xT[:, k, 0:T], ACT.Copy,
                                     scale=rest_sb[:, m, k:k + 1]).then_inc(part_ready[m], 1)

            def mixed_high(m, k, count):
                act.wait_ge(mixed_ready[m], count * KB - (KB - 1 - k))
                nc.scalar.copy(m_hi[m][:, k, :], mixed[m][k % 2][:]).then_inc(m_hi_ready[m], 1)

            def gather_xT(count):
                for k in range(KB):
                    act.wait_ge(xT_in_psum[k], count)
                    act.wait_ge(carried, count)
                    nc.scalar.copy(xT[:, k, 1:T + 1], xT_ps[k][:]).then_inc(xT_ready[k], 1)

            def mix_keys(count):
                part_of_previous(1, 0, count)
                for k in range(KB):
                    if k + 1 < KB:
                        part_of_previous(1, k + 1, count)
                    mixed_high(1, k, count)

            def step(n):
                part_of_previous(0, 0, n + 1)
                for k in range(KB):
                    if k + 1 < KB:
                        part_of_previous(0, k + 1, n + 1)
                    mixed_high(0, k, n + 1)
                    act.wait_ge(k_in_psum[k], n + 1)
                    nc.scalar.activation(k_relu[k % 2][:], k_ps[k % 2][:], ACT.Relu).then_inc(relu_done[k], 1)
                    if k >= 1:
                        act.wait_ge(square_done[k - 1], n + 1)
                        nc.scalar.copy(ka_hi[:, k - 1, :], k_square[(k - 1) % 2][:]).then_inc(ka_hi_ready[k - 1], 1)
                act.wait_ge(square_done[KB - 1], n + 1)
                nc.scalar.copy(ka_hi[:, KB - 1, :], k_square[(KB - 1) % 2][:]).then_inc(ka_hi_ready[KB - 1], 1)
                for j in range(J):
                    act.wait_ge(r_in_psum[j], n + 1)
                    act.wait_ge(gated_ready[j], n + 1)
                    nc.scalar.activation(gate[:, j, :], r_ps[j % 2][:], ACT.Sigmoid).then_inc(gate_ready[j], 1)
                gather_xT(n + 2)
                mix_keys(n + 2)

            def weights_high(w):
                nc.scalar.copy(w_hi[w][:, :, :], w_raw[w][:, :, :]).then_inc(w_hi_ready, 1)

            weights_high(WK)
            gather_xT(1)
            act.wait_ge(rest_ready, 1)
            mix_keys(1)
            weights_high(WR)
            weights_high(WV)
            with act.Fori(0, B) as b:
                for i in range(N):
                    step(b * N + i)

        @block.vector
        def _(dve):
            def mix(m, k, count):
                dve.wait_ge(part_ready[m], count * KB - (KB - 1 - k))
                if k >= 2:
                    dve.wait_ge(m_ready[m][k - 2], count)
                nc.vector.scalar_tensor_tensor(mixed[m][k % 2][:], xT[:, k, 1:T + 1], mu_sb[:, m, k:k + 1],
                                               part[m][k % 2][:], ALU.mult, ALU.add).then_inc(mixed_ready[m], 1)

            def mixed_low(m, k, count):
                dve.wait_ge(m_hi_ready[m], count * KB - (KB - 1 - k))
                nc.vector.tensor_tensor(m_lo[m][:, k, :], mixed[m][k % 2][:], m_hi[m][:, k, :].bitcast(F32),
                                        ALU.subtract).then_inc(m_ready[m][k], 1)

            def activation_low(k, count):
                dve.wait_ge(ka_hi_ready[k], count)
                nc.vector.tensor_tensor(ka_lo[:, k, :], k_square[k % 2][:], ka_hi[:, k, :].bitcast(F32),
                                        ALU.subtract).then_inc(ka_ready[k], 1)

            def apply_gate(j, n):
                dve.wait_ge(v_in_psum[j], n + 1)
                dve.wait_ge(gate_ready[j], n + 1 + (j >= 2))
                dve.wait_ge(result_ready[(j + 2) % 4], n + 1)
                nc.vector.tensor_tensor(gated[j % 2][:], v_ps[j % 2][:], gate[:, j, :], ALU.mult).then_inc(gated_ready[j], 1)

            def step(n, i, loads):
                mix(0, 0, n + 1)
                for k in range(KB):
                    if k + 1 < KB:
                        mix(0, k + 1, n + 1)
                    mixed_low(0, k, n + 1)
                    if 1 <= k < KB - 1:
                        activation_low(k - 1, n + 1)
                slot = (i + 1) % 2
                norm.statistics(dve, slot, loads)
                activation_low(KB - 2, n + 1)
                dve.wait_ge(norm.stats_done, n + 2)
                if i + 1 < N:
                    nc.vector.tensor_copy(xT[:, :, 0:1], xT[:, :, T:T + 1]).then_inc(carried, 1)
                else:
                    nc.vector.memset(xT[:, :, 0:1], 0.0).then_inc(carried, 1)
                norm.mean_and_variance()
                activation_low(KB - 1, n + 1)
                norm.normalize(dve, slot, n + 2)
                mix(1, 0, n + 2)
                mix(1, 1, n + 2)
                mixed_low(1, 0, n + 2)
                apply_gate(0, n)
                mix(1, 2, n + 2)
                mixed_low(1, 1, n + 2)
                apply_gate(1, n)
                mix(1, 3, n + 2)
                mixed_low(1, 2, n + 2)
                mixed_low(1, 3, n + 2)
                apply_gate(2, n)
                apply_gate(3, n)

            for j in range(J):
                dve.sem_inc(gated_ready[j], 1)
            nc.vector.memset(xT[:, :, 0:1], 0.0).then_inc(carried, 1)
            dve.wait_ge(mu_loaded, 16)
            nc.vector.tensor_scalar(rest_sb[:, :, :], mu_sb[:, :, :], -1.0, 1.0, ALU.mult, ALU.add).then_inc(rest_ready, 1)

            def weights_low(w, count):
                dve.wait_ge(w_hi_ready, count)
                nc.vector.tensor_tensor(w_lo[w][:, :, :], w_raw[w][:, :, :], w_hi[w][:, :, :].bitcast(F32),
                                        ALU.subtract).then_inc(w_lo_ready, 1)

            weights_low(WK, 1)
            mix(1, 0, 1)
            for k in range(KB):
                if k + 1 < KB:
                    mix(1, k + 1, 1)
                mixed_low(1, k, 1)
            weights_low(WR, 2)
            weights_low(WV, 3)
            with dve.Fori(0, B) as b:
                for i in range(N):
                    step(b * N + i, i, (b * (N // 2) + (i + 1) // 2) * 16 + 16)

        @block.gpsimd
        def _(pool):
            def step(n, i):
                for m in range(KB):
                    pool.wait_ge(relu_done[m], n + 1 + (m >= 2))
                    pool.wait_ge(ka_ready[(m + 2) % 4], n + 1)
                    nc.gpsimd.tensor_tensor(k_square[m % 2][:], k_relu[m % 2][:], k_relu[m % 2][:], ALU.mult).then_inc(square_done[m], 1)
                norm.inverse_deviation(pool, n + 2)
                for j in range(J):
                    pool.wait_ge(gated_ready[j], n + 2)
                    pool.wait_ge(stored[(j + 2) % 4], n * 16 + 16)
                    nc.gpsimd.tensor_tensor(result[j % 2][:], gated[j % 2][:], x1_sb[i % 2][:, j, :], ALU.add).then_inc(result_ready[j], 1)

            for i in (2, 3):
                pool.sem_inc(ka_ready[i], 1)
                pool.sem_inc(result_ready[i], 1)
                pool.sem_inc(stored[i], 16)
            with pool.Fori(0, B) as b:
                for i in range(N):
                    step(b * N + i, i)


def layer(nc, x, wq, wk, wv, wo, w_r, w_k, w_v, mu, tables, mask, tri, eye, out):
    B, L, _ = x.shape
    x1_dram = nc.dram_tensor("x1_dram", [B * L, C], F32, kind="Internal").ap()
    with ExitStack() as ctx:
        def sem(name):
            return ctx.enter_context(nc.semaphore(name))

        ffn_raw = [ctx.enter_context(nc.sbuf_tensor(f"ffn_raw{i}", [P, KB, C], F32)) for i in range(3)]
        norm = BlockNorm(ctx, nc, sem)
        attention_phase(nc, sem, norm, x, wq, wk, wv, wo, tables, mask, tri, eye, x1_dram, ffn_raw, [w_r, w_k, w_v])
        mix_phase(nc, sem, norm, x1_dram, ffn_raw, mu, out, L // 512)


def constants(length):
    theta = np.float32(10000.0)
    inv_freq = np.float32(1.0) / np.power(theta, np.arange(0, D, 2, dtype=np.float32) / np.float32(D), dtype=np.float32)
    angle = np.arange(length, dtype=np.float32)[:, None] * inv_freq[None, :]
    cos, sin = np.cos(angle), np.sin(angle)
    row = np.concatenate([np.repeat(cos, 2, axis=1), np.stack([-sin, sin], axis=-1).reshape(length, D)], axis=1)
    table = row.reshape(length // P, P, 2 * D).transpose(1, 0, 2)
    table = np.ascontiguousarray(np.concatenate([table, table[:, :1]], axis=1))
    at = np.arange(P)
    upto = (at[:, None] <= at[None, :]).astype(np.float32)
    after = np.float32(1.0) - upto
    return {"tables": table, "mask": upto, "tri": np.concatenate([upto, after], axis=1),
            "eye": np.eye(P, dtype=np.float32)}


def kernel(L0_attn_x, L0_attn_wq, L0_attn_wk, L0_attn_wv, L0_attn_wo, L0_ffn_W_r, L0_ffn_W_k, L0_ffn_W_v,
           L0_ffn_mu_r, L0_ffn_mu_k):
    import concourse.bacc as bacc
    from concourse.bass_utils import run_bass_kernel_spmd

    x = np.asarray(L0_attn_x)
    arrays = {
        "x": x, "wq": np.asarray(L0_attn_wq), "wk": np.asarray(L0_attn_wk), "wv": np.asarray(L0_attn_wv),
        "wo": np.asarray(L0_attn_wo),
        "w_r": np.asarray(L0_ffn_W_r).T, "w_k": np.asarray(L0_ffn_W_k).T, "w_v": np.asarray(L0_ffn_W_v).T,
        "mu": np.stack([np.asarray(L0_ffn_mu_r), np.asarray(L0_ffn_mu_k)]).reshape(2, KB, P).transpose(2, 0, 1),
        **constants(x.shape[1]),
    }
    arrays = {name: np.ascontiguousarray(a) for name, a in arrays.items()}
    nc = bacc.Bacc("TRN2", target_bir_lowering=False, num_devices=1)
    ins = {name: nc.dram_tensor(f"in_{name}", a.shape, F32, kind="ExternalInput").ap() for name, a in arrays.items()}
    out = nc.dram_tensor("out", x.shape, F32, kind="ExternalOutput").ap()
    layer(nc, out=out, **ins)
    got = run_bass_kernel_spmd(nc, [{f"in_{name}": a for name, a in arrays.items()}], core_ids=[0])
    return got.results[0]["out"]
```

```python
from contextlib import ExitStack

import numpy as np

import concourse.bass as bass
from concourse import mybir

F32 = mybir.dt.float32
F32R = mybir.dt.float32r
ALU = mybir.AluOpType
ACT = mybir.ActivationFunctionType
AX_X = mybir.AxisListType.X

P = 128
C = 512
KB = C // P
H = 16
D = C // H
HG = P // D
G = H // HG
UNROLL = 4
T = 512
J = T // P
WK, WQ, WV, WO, FK, FR, FV = range(7)
LN_EPS = 1e-5
DEN_EPS = 1e-6


class BlockNorm:

    def __init__(self, ctx, nc, sem):
        def sb(name, shape):
            return ctx.enter_context(nc.sbuf_tensor(name, shape, F32))

        self.nc = nc
        self.constants = sb("constants_sb", [P, 3, P])
        self.eye, self.upto = (self.constants[:, i, :] for i in range(2))
        self.power, self.epsilon, self.three_halves = sb("power", [P, J]), sb("epsilon", [P, J]), sb("three_halves", [P, J])
        self.x1 = [sb(f"x1_sb{i}", [P, J, C]) for i in range(2)]
        self.stats, self.mean_var = sb("f_stats", [P, J, 6]), sb("f_mean_var", [P, J, 2])
        self.rstd, self.xn = sb("f_rstd", [P, 4, J]), sb("f_xn", [P, J, C])
        self.x1_loaded = [sem(f"x1_loaded{i}") for i in range(2)]
        self.stats_done, self.meanvar_ready = sem("f_stats_done"), sem("f_meanvar_ready")
        self.rstd_step, self.rstd_ready, self.xn_ready = sem("f_rstd_step"), sem("f_rstd_ready"), sem("f_xn_ready")

    def statistics(self, dve, slot, loads):
        dve.wait_ge(self.x1_loaded[slot], loads)
        for j in range(J):
            last = self.nc.vector.bn_stats(self.stats[:, j, :], self.x1[slot][:, j, :])
        last.then_inc(self.stats_done, 1)

    def mean_and_variance(self):
        for j in range(J):
            last = self.nc.vector.bn_aggr(self.mean_var[:, j, :], self.stats[:, j, :])
        last.then_inc(self.meanvar_ready, 1)

    def normalize(self, dve, slot, count, tiles=range(J)):
        dve.wait_ge(self.rstd_ready, count)
        for j in tiles:
            last = self.nc.vector.tensor_scalar(self.xn[:, j, :], self.x1[slot][:, j, :], self.mean_var[:, j, 0:1],
                                                self.rstd[:, 3, j:j + 1], ALU.subtract, ALU.mult)
        if J - 1 in tiles:
            last.then_inc(self.xn_ready, 1)

    def inverse_deviation(self, pool, count):
        pool.wait_ge(self.meanvar_ready, count)
        inverse_square_root(self.nc, pool, self.mean_var[:, :, 1], [self.rstd[:, i, :] for i in range(4)],
                            self.power[:], self.epsilon[:], self.three_halves[:], self.rstd_step, self.rstd_ready, count)


def inverse_square_root(nc, pool, variance, columns, power, epsilon, three_halves, step, done, count):
    var, y, t, result = columns
    nc.gpsimd.tensor_tensor(var, variance, epsilon, ALU.add).then_inc(step, 1)
    pool.wait_ge(step, 6 * count - 5)
    nc.gpsimd.tensor_tensor(y, var, power, ALU.pow).then_inc(step, 1)
    pool.wait_ge(step, 6 * count - 4)
    nc.gpsimd.tensor_tensor(t, y, y, ALU.mult).then_inc(step, 1)
    pool.wait_ge(step, 6 * count - 3)
    nc.gpsimd.tensor_tensor(t, t, var, ALU.mult).then_inc(step, 1)
    pool.wait_ge(step, 6 * count - 2)
    nc.gpsimd.tensor_tensor(t, t, power, ALU.mult).then_inc(step, 1)
    pool.wait_ge(step, 6 * count - 1)
    nc.gpsimd.tensor_tensor(t, t, three_halves, ALU.add).then_inc(step, 1)
    pool.wait_ge(step, 6 * count)
    nc.gpsimd.tensor_tensor(result, t, y, ALU.mult).then_inc(done, 1)


class SplitWeights:

    def __init__(self, ctx, nc, sem, matrices):
        self.nc, self.matrices, self.raw = nc, matrices, {}
        self.hi = [ctx.enter_context(nc.sbuf_tensor(f"w_hi{i}", [P, KB, C], F32R)) for i in range(4)]
        self.lo = [ctx.enter_context(nc.sbuf_tensor(f"w_lo{i}", [P, KB, C], F32R)) for i in range(4)]
        self.loaded = [[sem(f"w_loaded{i}{j}") for j in range(2)] for i in range(4)]
        self.hi_ready, self.lo_ready = sem("w_hi_ready"), sem("w_lo_ready")

    def load(self, sp, i):
        for k in range(KB):
            sp.dma_start(self.raw[i][k], self.matrices[i][k * P:(k + 1) * P, :]).then_inc(self.loaded[i % 4][k // 2], 16)

    def high(self, act, i, k):
        act.wait_ge(self.loaded[i % 4][k // 2], 32 * (i // 4 + 1))
        self.nc.scalar.copy(self.hi[i % 4][:, k, :], self.raw[i][k]).then_inc(self.hi_ready, 1)

    def low(self, engine, operations, i, k):
        engine.wait_ge(self.hi_ready, i * KB + k + 1)
        operations.tensor_tensor(self.lo[i % 4][:, k, :], self.raw[i][k], self.hi[i % 4][:, k, :].bitcast(F32),
                                 ALU.subtract).then_inc(self.lo_ready, 1)


class KeyMix:

    def __init__(self, ctx, nc, sem):
        def sb(name, shape, dt=F32):
            return ctx.enter_context(nc.sbuf_tensor(name, shape, dt))

        self.nc = nc
        self.mu = sb("mu_sb", [P, 2, KB])
        self.rest = sb("rest_sb", [P, 2, KB])
        self.xT = sb("xT", [P, KB, T + 1])
        self.m_hi, self.m_lo = [None, sb("m_hi1", [P, KB, T], F32R)], [None, sb("m_lo1", [P, KB, T], F32R)]
        self.part = self.mixed = None
        self.mu_loaded, self.rest_ready, self.carried = sem("mu_loaded"), sem("rest_ready"), sem("carried")
        self.xT_in_psum, self.xT_ready = [[sem(f"{name}{k}") for k in range(KB)] for name in ("xT_in_psum", "xT_ready")]
        self.m_ready = [[sem(f"m_{name}{k}") for k in range(KB)] for name in ("r", "k")]
        self.part_ready, self.mixed_ready, self.m_hi_ready = [[sem(f"{name}_r"), sem(f"{name}_k")] for name in ("part", "mixed", "m_hi")]

    def gather(self, act, psum, k, count):
        act.wait_ge(self.xT_in_psum[k], count)
        act.wait_ge(self.carried, count)
        self.nc.scalar.copy(self.xT[:, k, 1:T + 1], psum[:]).then_inc(self.xT_ready[k], 1)

    def part_of_previous(self, act, m, k, count):
        act.wait_ge(self.xT_ready[k], count)
        self.nc.scalar.activation(self.part[m][k % 2][:], self.xT[:, k, 0:T], ACT.Copy,
                                  scale=self.rest[:, m, k:k + 1]).then_inc(self.part_ready[m], 1)

    def high(self, act, m, k, count):
        act.wait_ge(self.mixed_ready[m], count * KB - (KB - 1 - k))
        self.nc.scalar.copy(self.m_hi[m][:, k, :], self.mixed[m][k % 2][:]).then_inc(self.m_hi_ready[m], 1)

    def mix(self, dve, m, k, count):
        dve.wait_ge(self.part_ready[m], count * KB - (KB - 1 - k))
        if k >= 2:
            dve.wait_ge(self.m_ready[m][k - 2], count)
        self.nc.vector.scalar_tensor_tensor(self.mixed[m][k % 2][:], self.xT[:, k, 1:T + 1], self.mu[:, m, k:k + 1],
                                            self.part[m][k % 2][:], ALU.mult, ALU.add).then_inc(self.mixed_ready[m], 1)

    def low(self, dve, m, k, count):
        dve.wait_ge(self.m_hi_ready[m], count * KB - (KB - 1 - k))
        self.nc.vector.tensor_tensor(self.m_lo[m][:, k, :], self.mixed[m][k % 2][:], self.m_hi[m][:, k, :].bitcast(F32),
                                     ALU.subtract).then_inc(self.m_ready[m][k], 1)


def within(tile, ahead, tiles):
    return not isinstance(tile, int) or tile + ahead < tiles


def attention_phase(nc, sem, norm, weights, mixer, x, mu, tables, consts, x1_dram):
    B, L, _ = x.shape
    tiles = B * L // P
    per_batch = L // P
    inner = per_batch // UNROLL
    x_tiles = x.rearrange("b (n p) c -> (b n) p c", p=P)
    x1_tiles = x1_dram.rearrange("(n p) c -> n p c", p=P)
    x1_blocks = x1_dram.rearrange("(n j p) c -> n p j c", p=P, j=J)
    eye = norm.eye

    with ExitStack() as ctx:
        def sb(name, shape, dt=F32):
            return ctx.enter_context(nc.sbuf_tensor(name, shape, dt))

        def bank(name):
            return ctx.enter_context(nc.psum_tensor(name, [P, 512], F32))

        w_hi, w_lo = weights.hi, weights.lo
        table_sb = sb("table_sb", [P, per_batch + 1, 2 * D])
        sums_r = sb("sums_r", [P, 2, P], F32R)
        sum_upto, sum_carried = sums_r[:, 0, :], sums_r[:, 1, :]
        zeros_r = sb("zeros_r", [P, C], F32R)
        x_sb = [sb(f"x_sb{u}", [P, C]) for u in range(UNROLL)]
        stats = [sb(f"stats{u}", [P, 6]) for u in range(2)]
        mean_var = [sb(f"mean_var{u}", [P, 2]) for u in range(2)]
        rstd = [sb(f"rstd{u}", [P, 4]) for u in range(2)]
        xn = sb("xn", [P, C])
        xnT_hi = [sb(f"xnT_hi{u}", [P, KB, P], F32R) for u in range(2)]
        xnT_lo = [sb(f"xnT_lo{u}", [P, KB, P], F32R) for u in range(2)]
        k_cos, k_sin, k_sum = sb("k_cos", [P, C]), sb("k_sin", [P, C]), sb("k_sum", [P, C])
        q_cos, q_sin, q_sum = sb("q_cos", [P, C]), sb("q_sin", [P, C]), sb("q_sum", [P, C])
        k_nat = [sb(f"k_nat{u}", [P, C]) for u in range(2)]
        k_hi, k_lo = sb("k_hi", [P, C], F32R), sb("k_lo", [P, C], F32R)
        carry_raw, carry = sb("carry_raw", [P, C]), sb("carry", [P, C], F32R)
        q_nat, q_norm, v_nat = sb("q_nat", [P, C]), sb("q_norm", [P, C]), sb("v_nat", [P, C])
        prod = sb("prod", [P, C])
        den = sb("den", [P, 3, H])
        kT_pair = [sb(f"kT_pair{i}", [P, G, P], F32R) for i in range(2)]
        qT = sb("qT", [P, G, P])
        qx_hi = [sb(f"qx_hi{i}", [P, G, 2, P], F32R) for i in range(2)]
        qx_lo = [sb(f"qx_lo{i}", [P, G, 2, P], F32R) for i in range(2)]
        probs = sb("probs", [P, G, HG * P])
        state = sb("state", [P, G, P])
        oT_hi, oT_lo = sb("oT_hi", [P, G, P], F32R), sb("oT_lo", [P, G, P], F32R)

        bank0, bank1, bank2, bank3 = bank("bank0"), bank("bank1"), bank("bank2"), bank("bank3")
        bank4, bank5, kcum, kv = bank("bank4"), bank("bank5"), bank("kcum"), bank("kv")
        xnT_ps, outT_ps = bank2, bank0
        attn_ps = bank1
        kT_ps, qT_ps = bank2, bank5
        k_ps, v_ps, q_ps = bank3, bank3, bank4
        score_ps = [bank0, bank1, bank2, bank5]

        consts_loaded, table_loaded, tables_loaded = sem("consts_loaded"), sem("table_loaded"), sem("tables_loaded")
        sums_ready, consts_set, zeros_set = sem("sums_ready"), sem("consts_set"), sem("zeros_set")
        x_loaded = [sem(f"x_loaded{u}") for u in range(UNROLL)]
        x1_stored = [sem(f"x1_stored{u}") for u in range(UNROLL)]
        stats_done, meanvar_ready, rstd_ready = sem("stats_done"), sem("meanvar_ready"), sem("rstd_ready")
        rstd_step = sem("rstd_step")
        xn_ready = sem("xn_ready")
        xnT_in_psum, xnT_hi_ready, xnT_ready = sem("xnT_in_psum"), sem("xnT_hi_ready"), sem("xnT_ready")
        k_in_psum, q_in_psum, v_in_psum = sem("k_in_psum"), sem("q_in_psum"), sem("v_in_psum")
        k_rotated, q_rotated = sem("k_rotated"), sem("q_rotated")
        k_summed, q_summed = sem("k_summed"), sem("q_summed")
        k_ready, k_hi_ready, k_split = sem("k_ready"), sem("k_hi_ready"), sem("k_split")
        q_ready, v_ready = sem("q_ready"), sem("v_ready")
        kcum_ready, kcum_used = sem("kcum_ready"), sem("kcum_used")
        carry_copied, carry_hi_ready, carry_ready = sem("carry_copied"), sem("carry_hi_ready"), sem("carry_ready")
        den_step, q_normed = sem("den_step"), sem("q_normed")
        kT_in_psum, kT_ready = sem("kT_in_psum"), sem("kT_ready")
        kT_hi_ready = [sem(f"kT_hi_ready{i}") for i in range(2)]
        qT_in_psum, qx_ready, qT_ready = sem("qT_in_psum"), sem("qx_ready"), sem("qT_ready")
        qx_doubled = [sem(f"qx_doubled{i}") for i in range(2)]
        qx_hi_ready = sem("qx_hi_ready")
        kv_ready, state_ready = sem("kv_ready"), sem("state_ready")
        scores_ready = [sem(f"scores_ready{g}") for g in range(G)]
        scores_free = [sem(f"scores_free{g}") for g in range(G)]
        outT_in_psum, oT_hi_ready, oT_ready = sem("outT_in_psum"), sem("oT_hi_ready"), sem("oT_ready")
        attn_ready, x1_ready = sem("attn_ready"), sem("x1_ready")

        block = ctx.enter_context(nc.Block())

        half = [slice(0, P // 2), slice(P // 2, P)]

        def heads(ap):
            return ap.rearrange("p (h d) -> p h d", d=D)

        weights.raw = {WK: [norm.x1[0][:, k, :] for k in range(KB)], WQ: [norm.x1[1][:, k, :] for k in range(KB)],
                       WV: [norm.xn[:, k, :] for k in range(KB)], WO: [probs[:, k, :] for k in range(KB)],
                       FK: [norm.x1[1][:, k, :] for k in range(KB)],
                       FR: [k_sum[:], q_sum[:], xn[:], table_sb[:, 0:C // (2 * D), :].rearrange("p a b -> p (a b)")],
                       FV: [norm.xn[:, k, :] for k in range(KB)]}
        mixer.part, mixer.mixed = [None, [k_cos, k_sin]], [None, [q_cos, q_sin]]
        xT_ps = [bank3, bank4]

        def split3(psum, lhs_hi, lhs_lo, rhs_hi, rhs_lo, start, stop):
            nc.tensor.matmul(psum, lhs_hi, rhs_hi, start=start, stop=False)
            nc.tensor.matmul(psum, lhs_lo, rhs_hi, start=False, stop=False)
            return nc.tensor.matmul(psum, lhs_hi, rhs_lo, start=False, stop=stop)

        @block.sync
        def _(sp):
            sp.dma_start(x_sb[0][:], x_tiles[0, :, :]).then_inc(x_loaded[0], 16)
            sp.dma_start(norm.constants[:, :, :], consts).then_inc(consts_loaded, 16)
            weights.load(sp, WK)
            sp.dma_start(x_sb[1][:], x_tiles[1, :, :]).then_inc(x_loaded[1], 16)
            weights.load(sp, WQ)
            sp.dma_start(table_sb[:, 0:1, :], tables[:, 0:1, :]).then_inc(table_loaded, 16)
            weights.load(sp, WV)
            sp.dma_start(table_sb[:, 1:, :], tables[:, 1:, :]).then_inc(tables_loaded, 16)
            sp.dma_start(x_sb[2][:], x_tiles[2, :, :]).then_inc(x_loaded[2], 16)
            weights.load(sp, WO)
            sp.dma_start(x_sb[3][:], x_tiles[3, :, :]).then_inc(x_loaded[3], 16)
            sp.dma_start(mixer.mu[:, :, :], mu).then_inc(mixer.mu_loaded, 16)

            def store(tile, turn, u):
                sp.wait_ge(x1_ready, tile + 2)
                sp.dma_start(x1_tiles[bass.ds(tile, 1), :, :].rearrange("o p c -> (o p) c"),
                             x_sb[u][:]).then_inc(x1_stored[u], 16)
                sp.wait_ge(x1_stored[u], 16 * turn + 16)

            def turns(first, last):
                with sp.Fori(first, last) as turn:
                    for u in range(UNROLL):
                        tile = turn * UNROLL + u
                        store(tile, turn, u)
                        sp.dma_start(x_sb[u][:], x_tiles[bass.ds(tile + UNROLL, 1), :, :].rearrange("o p c -> (o p) c")).then_inc(x_loaded[u], 16)

            turns(0, inner)
            sp.wait_ge(weights.lo_ready, 4 * KB)
            sp.dma_start(norm.x1[0][:, :, :], x1_blocks[0, :, :, :]).then_inc(norm.x1_loaded[0], 16)
            turns(inner, tiles // UNROLL - 1)
            for u in range(UNROLL):
                if u == UNROLL - 2:
                    sp.wait_ge(k_in_psum, tiles)
                    weights.load(sp, FK)
                store(tiles - UNROLL + u, tiles // UNROLL - 1, u)
                if u == UNROLL - 2:
                    for done in (q_in_psum, k_ready, q_ready, xnT_in_psum, k_rotated, q_rotated):
                        sp.wait_ge(done, tiles)
                    weights.load(sp, FR)
                    sp.wait_ge(weights.lo_ready, 5 * KB)
                    sp.dma_start(norm.x1[1][:, :, :], x1_blocks[1, :, :, :]).then_inc(norm.x1_loaded[1], 16)
                    sp.wait_ge(v_in_psum, tiles)
                    sp.wait_ge(mixer.xT_in_psum[KB - 1], 1)
                    weights.load(sp, FV)

        @block.tensor
        def _(pe):
            def transpose_xn():
                for k in range(KB):
                    last = nc.tensor.transpose(xnT_ps[:, k * P:(k + 1) * P], xn[:, k * P:(k + 1) * P], eye)
                last.then_inc(xnT_in_psum, 1)

            def project(psum, slot, w, blocks=range(KB)):
                for k in blocks:
                    last = split3(psum[:], xnT_hi[slot][:, k, :], xnT_lo[slot][:, k, :],
                                  w_hi[w][:, k, :], w_lo[w][:, k, :], k == 0, k == KB - 1)
                return last

            def keep_clock_up(products):
                for _ in range(products):
                    nc.tensor.matmul(kv[:], zeros_r[:, 0:P], zeros_r[:], start=True, stop=True, skip_group_check=True)

            def transpose_block(features, tile):
                for k in features:
                    if k == 0:
                        pe.wait_ge(norm.xn_ready, 1)
                        pe.wait_ge(v_ready, tile + 1)
                    elif k == 1:
                        pe.wait_ge(q_rotated, tile + 1)
                    else:
                        pe.wait_ge(mixer.xT_ready[k - 2], 1)
                    for j in range(J):
                        last = nc.tensor.transpose(xT_ps[k % 2][:, j * P:(j + 1) * P], norm.xn[:, j, k * P:(k + 1) * P], eye)
                    last.then_inc(mixer.xT_in_psum[k], 1)

            def step(b, tile, u):
                ahead, here = (u + 1) % 2, u % 2
                pe.wait_ge(carry_ready, tile + b + 1)
                pe.wait_ge(k_split, tile + 1)
                nc.tensor.matmul(kcum[:], sum_carried, carry[:], start=True, stop=False)
                nc.tensor.matmul(kcum[:], sum_upto, k_hi[:], start=False, stop=False)
                nc.tensor.matmul(kcum[:], sum_upto, k_lo[:], start=False, stop=True).then_inc(kcum_ready, 1)
                pe.wait_ge(k_ready, tile + 1)
                if within(tile, 1, tiles):
                    pe.wait_ge(xnT_ready, tile + 2)
                for g in range(G):
                    last = nc.tensor.transpose(kT_ps[:, g * P:(g + 1) * P], k_nat[here][:, g * P:(g + 1) * P], eye)
                last.then_inc(kT_in_psum, 1)
                if within(tile, 1, tiles):
                    pe.wait_ge(v_ready, tile + 1)
                    project(k_ps, ahead, WK).then_inc(k_in_psum, 1)
                else:
                    transpose_block(range(0, 2), tile)
                    pe.wait_ge(state_ready, tile + 1)
                    keep_clock_up(8)
                pe.wait_ge(q_normed, tile + 1)
                pe.wait_ge(scores_free[3], tile + 1)
                for g in range(G):
                    last = nc.tensor.transpose(qT_ps[:, g * P:(g + 1) * P], q_norm[:, g * P:(g + 1) * P], eye)
                last.then_inc(qT_in_psum, 1)
                if within(tile, 1, tiles):
                    pe.wait_ge(q_rotated, tile + 1)
                    project(q_ps, ahead, WQ).then_inc(q_in_psum, 1)
                    pe.wait_ge(k_rotated, tile + 2)
                    project(v_ps, ahead, WV, range(KB - 1))
                else:
                    transpose_block(range(2, 4), tile)
                    keep_clock_up(11)
                pe.wait_ge(kT_ready, tile + 1)
                pe.wait_ge(qx_ready, tile + 1)
                pe.wait_ge(x1_ready, tile + 1)
                for g in range(G):
                    if g == G - 1:
                        pe.wait_ge(qT_ready, tile + 1)
                    for i in range(2):
                        pair_ps = score_ps[g][:, i * 2 * P:(i + 1) * 2 * P]
                        nc.tensor.matmul(pair_ps, kT_pair[i][:, g, :], qx_lo[i][:, g, :, :].rearrange("p a b -> p (a b)"),
                                         start=True, stop=False, skip_group_check=True)
                        if g == 0:
                            pe.wait_ge(qx_doubled[i], tile + 1)
                        last = nc.tensor.matmul(pair_ps, kT_pair[i][:, g, :], qx_hi[i][:, g, :, :].rearrange("p a b -> p (a b)"),
                                                start=False, stop=True, skip_group_check=True)
                    last.then_inc(scores_ready[g], 1)
                pe.wait_ge(scores_free[0], tile + 2)
                for g in range(G):
                    nc.tensor.matmul(outT_ps[:, g * P:(g + 1) * P], state[:, g, :], qT[:, g, :],
                                     start=(g == 0), stop=False, skip_group_check=True)
                for g in range(G):
                    pe.wait_ge(scores_free[g], tile + 2)
                    for h in range(HG):
                        f = g * P + h * D
                        last = nc.tensor.matmul(outT_ps[h * D:(h + 1) * D, g * P:(g + 1) * P], v_nat[:, f:f + D],
                                                probs[:, g, h * P:(h + 1) * P], start=False,
                                                stop=(g == G - 1 and h == HG - 1), skip_group_check=True)
                last.then_inc(outT_in_psum, 1)
                if within(tile, 1, tiles):
                    pe.wait_ge(state_ready, tile + 1)
                    for g in range(G):
                        for h in range(HG):
                            f = g * P + h * D
                            last = nc.tensor.matmul(kv[h * D:(h + 1) * D, g * D:(g + 1) * D], k_nat[here][:, f:f + D],
                                                    v_nat[:, f:f + D], start=False, stop=True, skip_group_check=True)
                    last.then_inc(kv_ready, 1)
                    project(v_ps, ahead, WV, range(KB - 1, KB)).then_inc(v_in_psum, 1)
                if within(tile, 2, tiles):
                    pe.wait_ge(xn_ready, tile + 3)
                    transpose_xn()
                if not within(tile, 1, tiles):
                    keep_clock_up(7)
                pe.wait_ge(weights.lo_ready, 4 * KB)
                pe.wait_ge(oT_ready, tile + 2)
                for g in range(G):
                    last = split3(attn_ps[:], oT_hi[:, g, :], oT_lo[:, g, :], w_hi[WO][:, g, :], w_lo[WO][:, g, :],
                                  g == 0, g == G - 1)
                last.then_inc(attn_ready, 1)

            pe.wait_ge(consts_set, 1)
            keep_clock_up(11)
            pe.wait_ge(consts_loaded, 16)
            pe.wait_ge(xn_ready, 1)
            transpose_xn()
            pe.wait_ge(xnT_ready, 1)

            def first_project(psum, w):
                for k in range(KB):
                    pe.wait_ge(weights.lo_ready, w * KB + k + 1)
                    last = split3(psum[:], xnT_hi[0][:, k, :], xnT_lo[0][:, k, :],
                                  w_hi[w][:, k, :], w_lo[w][:, k, :], k == 0, k == KB - 1)
                return last

            first_project(k_ps, WK).then_inc(k_in_psum, 1)
            first_project(q_ps, WQ).then_inc(q_in_psum, 1)
            pe.wait_ge(xn_ready, 2)
            transpose_xn()
            pe.wait_ge(k_rotated, 1)
            first_project(v_ps, WV).then_inc(v_in_psum, 1)
            pe.wait_ge(sums_ready, 1)

            def empty_sum():
                nc.tensor.matmul(kv[:], zeros_r[:, 0:P], zeros_r[:], start=True, stop=True,
                                 skip_group_check=True).then_inc(kv_ready, 1)

            with pe.Fori(0, B - 1) as b:
                empty_sum()
                with pe.Fori(0, inner) as turn:
                    for u in range(UNROLL):
                        step(b, b * per_batch + turn * UNROLL + u, u)
            empty_sum()
            with pe.Fori(0, inner - 1) as turn:
                for u in range(UNROLL):
                    step(B - 1, (B - 1) * per_batch + turn * UNROLL + u, u)
            for u in range(UNROLL):
                step(B - 1, tiles - UNROLL + u, u)
            keep_clock_up(16)

        @block.scalar
        def _(act):
            def xnT_high(slot, count):
                act.wait_ge(xnT_in_psum, count)
                nc.scalar.copy(xnT_hi[slot][:, :, :].rearrange("p k n -> p (k n)"), xnT_ps[:]).then_inc(xnT_hi_ready, 1)

            def keys(slot, count):
                act.wait_ge(k_summed, count)
                nc.scalar.activation(k_nat[slot][:], k_sum[:], ACT.Relu).then_inc(k_ready, 1)
                act.wait_ge(k_ready, count)
                nc.scalar.copy(k_hi[:], k_nat[slot][:]).then_inc(k_hi_ready, 1)

            def queries(count):
                act.wait_ge(q_summed, count)
                nc.scalar.activation(q_nat[:], q_sum[:], ACT.Relu).then_inc(q_ready, 1)

            def values(count):
                act.wait_ge(v_in_psum, count)
                nc.scalar.copy(v_nat[:], v_ps[:]).then_inc(v_ready, 1)

            def step(b, tile, u):
                last_tile = not within(tile, 1, tiles)
                act.wait_ge(kT_in_psum, tile + 1)
                for i in range(2):
                    nc.scalar.copy(kT_pair[i][half[i], :, :].rearrange("p g n -> p (g n)"),
                                   kT_ps[half[i], :]).then_inc(kT_hi_ready[i], 1)
                act.wait_ge(kv_ready, tile + b + 1)
                for q in range(HG):
                    own = slice(q * D, (q + 1) * D)
                    last = nc.scalar.copy(state[own, :, own], kv[own, 0:G * D].rearrange("p (g n) -> p g n", g=G))
                last.then_inc(state_ready, 1)
                if not last_tile:
                    act.wait_ge(kcum_used, tile + 1)
                    nc.scalar.copy(carry_raw[P - D:P, :], kcum[P - D:P, :]).then_inc(carry_copied, 1)
                    act.wait_ge(carry_copied, tile + 1)
                    nc.scalar.copy(carry[P - D:P, :], carry_raw[P - D:P, :]).then_inc(carry_hi_ready, 1)
                if last_tile:
                    for k in range(2):
                        mixer.gather(act, xT_ps[k], k, 1)
                    for k in range(2):
                        mixer.part_of_previous(act, 1, k, 1)
                act.wait_ge(qT_in_psum, tile + 1)
                for q in range(HG):
                    own = slice(q * D, (q + 1) * D)
                    nc.scalar.copy(qx_hi[q // 2][own, :, q % 2, :],
                                   qT_ps[own, :].rearrange("p (g n) -> p g n", g=G)).then_inc(qx_hi_ready, 1)
                for q in range(HG):
                    own, other = slice(q * D, (q + 1) * D), slice((q + 2) % 4 * D, ((q + 2) % 4 + 1) * D)
                    act.wait_ge(qx_hi_ready, HG * tile + q + 1)
                    last = nc.scalar.copy(qx_hi[q // 2][other, :, q % 2, :], qx_hi[q // 2][own, :, q % 2, :])
                    if q % 2:
                        last.then_inc(qx_doubled[q // 2], 1)
                act.wait_ge(qx_ready, tile + 1)
                nc.scalar.copy(qT[:, :, :].rearrange("p g n -> p (g n)"), qT_ps[:]).then_inc(qT_ready, 1)
                if last_tile:
                    for k in range(2, 4):
                        mixer.gather(act, xT_ps[k % 2], k, 1)
                    for k in range(2):
                        mixer.high(act, 1, k, 1)
                    for k in range(2, 4):
                        mixer.part_of_previous(act, 1, k, 1)
                    for k in range(2):
                        weights.high(act, FR, k)
                else:
                    act.wait_ge(kcum_ready, tile + 1)
                    keys((u + 1) % 2, tile + 2)
                    act.wait_ge(q_normed, tile + 1)
                    queries(tile + 2)
                act.wait_ge(outT_in_psum, tile + 1)
                nc.scalar.copy(oT_hi[:, :, :].rearrange("p g n -> p (g n)"), outT_ps[:]).then_inc(oT_hi_ready, 1)
                if last_tile:
                    for k in range(2, 4):
                        weights.high(act, FR, k)
                    for k in range(2, 4):
                        mixer.high(act, 1, k, 1)
                else:
                    values(tile + 2)
                if within(tile, 2, tiles):
                    xnT_high(u % 2, tile + 3)
                elif not last_tile:
                    for k in range(KB):
                        weights.high(act, FK, k)

            weights.high(act, WK, 0)
            xnT_high(0, 1)
            for k in range(1, KB):
                weights.high(act, WK, k)
            for w in (WQ, WV):
                for k in range(KB):
                    weights.high(act, w, k)
            xnT_high(1, 2)
            act.wait_ge(consts_loaded, 16)
            nc.scalar.copy(sums_r[:, :, :], norm.constants[:, 1:3, :]).then_inc(sums_ready, 1)
            keys(0, 1)
            values(1)
            for k in range(KB):
                weights.high(act, WO, k)
            queries(1)
            act.wait_ge(consts_set, 1)
            act.wait_ge(zeros_set, 1)
            with act.Fori(0, B - 1) as b:
                with act.Fori(0, inner) as turn:
                    for u in range(UNROLL):
                        step(b, b * per_batch + turn * UNROLL + u, u)
                act.wait_ge(carry_ready, (b + 1) * (per_batch + 1))
                nc.scalar.copy(carry[P - 2 * D:P, :], zeros_r[P - 2 * D:P, :].bitcast(F32)).then_inc(carry_ready, 1)
            with act.Fori(0, inner - 1) as turn:
                for u in range(UNROLL):
                    step(B - 1, (B - 1) * per_batch + turn * UNROLL + u, u)
            act.wait_ge(mixer.rest_ready, 1)
            for u in range(UNROLL):
                step(B - 1, tiles - UNROLL + u, u)

        @block.vector
        def _(dve):
            def normalize_stats(slot, loads):
                dve.wait_ge(x_loaded[slot], loads)
                nc.vector.bn_stats(stats[slot % 2][:], x_sb[slot][:]).then_inc(stats_done, 1)

            def mean_and_variance(slot):
                nc.vector.bn_aggr(mean_var[slot % 2][:], stats[slot % 2][:]).then_inc(meanvar_ready, 1)

            def normalize(slot, count):
                dve.wait_ge(rstd_ready, count)
                nc.vector.tensor_scalar(xn[:], x_sb[slot][:], mean_var[slot % 2][:, 0:1], rstd[slot % 2][:, 3:4],
                                        ALU.subtract, ALU.mult).then_inc(xn_ready, 1)

            def xnT_low(slot, count):
                dve.wait_ge(xnT_hi_ready, count)
                nc.vector.tensor_tensor(xnT_lo[slot][:, :, :].rearrange("p k n -> p (k n)"), xnT_ps[:],
                                        xnT_hi[slot][:, :, :].rearrange("p k n -> p (k n)").bitcast(F32),
                                        ALU.subtract).then_inc(xnT_ready, 1)

            def rotate(psum, by_cos, by_sin, position, done):
                pair = table_sb[:, bass.ds(position, 1), :] if not isinstance(position, int) else table_sb[:, position:position + 1, :]
                cos = pair[:, :, 0:D].broadcast_to([P, H, D])
                sin = pair[:, :, D:2 * D].rearrange("p o (f c) -> p o f c", c=2).broadcast_to([P, H, D // 2, 2])
                nc.vector.tensor_tensor(heads(by_cos[:]), heads(psum[:]), cos, ALU.mult)
                swapped = psum[:].rearrange("p (h f c) -> p h f c", h=H, c=2)[:, :, :, ::-1]
                nc.vector.tensor_tensor(by_sin[:].rearrange("p (h f c) -> p h f c", h=H, c=2), swapped, sin,
                                        ALU.mult).then_inc(done, 1)

            def step(turn, tile, all_turn, u):
                last_tile = not within(tile, 1, tiles)
                dve.wait_ge(q_ready, tile + 1)
                dve.wait_ge(kcum_ready, tile + 1)
                nc.vector.tensor_tensor(prod[:], q_nat[:], kcum[:], ALU.mult).then_inc(kcum_used, 1)
                dve.wait_ge(kcum_used, tile + 1)
                nc.vector.tensor_reduce(den[:, 0, :], heads(prod[:]), AX_X, ALU.add).then_inc(den_step, 1)
                dve.wait_ge(den_step, 3 * tile + 1)
                nc.vector.tensor_scalar_add(den[:, 1, :], den[:, 0, :], DEN_EPS).then_inc(den_step, 1)
                dve.wait_ge(den_step, 3 * tile + 2)
                nc.vector.reciprocal(den[:, 2, :], den[:, 1, :]).then_inc(den_step, 1)
                dve.wait_ge(den_step, 3 * tile + 3)
                nc.vector.tensor_tensor(heads(q_norm[:]), heads(q_nat[:]),
                                        den[:, 2, :].rearrange("p (h o) -> p h o", o=1).broadcast_to([P, H, D]),
                                        ALU.mult).then_inc(q_normed, 1)
                for i in range(2):
                    dve.wait_ge(kT_hi_ready[i], tile + 1)
                    last = nc.vector.tensor_tensor(kT_pair[i][half[1 - i], :, :].rearrange("p g n -> p (g n)"), kT_ps[half[i], :],
                                                   kT_pair[i][half[i], :, :].rearrange("p g n -> p (g n)").bitcast(F32),
                                                   ALU.subtract)
                last.then_inc(kT_ready, 1)
                if not last_tile:
                    dve.wait_ge(k_in_psum, tile + 2)
                    dve.wait_ge(k_summed, tile + 1)
                    rotate(k_ps, k_cos, k_sin, turn * UNROLL + u + 1, k_rotated)
                for q in range(HG):
                    own = slice(q * D, (q + 1) * D)
                    dve.wait_ge(qx_hi_ready, HG * tile + q + 1)
                    last = nc.vector.tensor_tensor(qx_lo[q // 2][own, :, q % 2, :], qT_ps[own, :].rearrange("p (g n) -> p g n", g=G),
                                                   qx_hi[q // 2][own, :, q % 2, :].bitcast(F32), ALU.subtract)
                last.then_inc(qx_ready, 1)
                if last_tile:
                    for k in range(2):
                        mixer.mix(dve, 1, k, 1)
                else:
                    dve.wait_ge(q_in_psum, tile + 2)
                    dve.wait_ge(q_summed, tile + 1)
                    rotate(q_ps, q_cos, q_sin, turn * UNROLL + u + 1, q_rotated)
                dve.wait_ge(weights.lo_ready, 4 * KB)
                for g in range(G):
                    dve.wait_ge(scores_ready[g], tile + 1)
                    nc.vector.tensor_tensor(probs[:, g, :].rearrange("p (h n) -> p h n", h=HG),
                                            score_ps[g][:].rearrange("p (h n) -> p h n", h=HG),
                                            norm.upto.rearrange("p (o n) -> p o n", o=1).broadcast_to([P, HG, P]),
                                            ALU.mult).then_inc(scores_free[g], 1)
                if within(tile, 2, tiles):
                    normalize((u + 2) % UNROLL, tile + 3)
                if last_tile:
                    for k in range(2):
                        mixer.low(dve, 1, k, 1)
                else:
                    dve.wait_ge(carry_hi_ready, tile + 1)
                    nc.vector.tensor_tensor(carry[P - 2 * D:P - D, :], carry_raw[P - D:P, :], carry[P - D:P, :].bitcast(F32),
                                            ALU.subtract).then_inc(carry_ready, 1)
                dve.wait_ge(oT_hi_ready, tile + 1)
                nc.vector.tensor_tensor(oT_lo[:, :, :].rearrange("p g n -> p (g n)"), outT_ps[:],
                                        oT_hi[:, :, :].rearrange("p g n -> p (g n)").bitcast(F32),
                                        ALU.subtract).then_inc(oT_ready, 1)
                if within(tile, 3, tiles):
                    normalize_stats((u + 3) % UNROLL, 16 * all_turn + (16 if u == 0 else 32))
                    dve.wait_ge(stats_done, tile + 4)
                if within(tile, 2, tiles):
                    xnT_low(u % 2, tile + 3)
                if within(tile, 3, tiles):
                    mean_and_variance((u + 3) % UNROLL)
                if isinstance(tile, int) and not last_tile:
                    norm.normalize(dve, 0, 1, range(u, u + 1) if u < 2 else range(2, 4))
                    if u == UNROLL - 2:
                        for k in range(KB):
                            weights.low(dve, nc.vector, FK, k)
                if last_tile:
                    for k in range(2, 4):
                        mixer.mix(dve, 1, k, 1)
                    weights.low(dve, nc.vector, FR, 0)
                    for k in range(2, 4):
                        mixer.low(dve, 1, k, 1)
                dve.wait_ge(attn_ready, tile + 1)
                nc.vector.tensor_tensor(x_sb[u][:], x_sb[u][:], attn_ps[:], ALU.add).then_inc(x1_ready, 1)
                if last_tile:
                    for k in range(1, KB):
                        weights.low(dve, nc.vector, FR, k)

            nc.vector.memset(norm.power[:], -0.5)
            nc.vector.memset(norm.epsilon[:], LN_EPS)
            nc.vector.memset(norm.three_halves[:], 1.5)
            nc.vector.memset(state[:, :, :], 0.0)
            nc.vector.memset(zeros_r[:].bitcast(F32), 0.0).then_inc(consts_set, 1)
            def first_stats(u):
                normalize_stats(u, 16)
                dve.wait_ge(stats_done, u + 1)
                mean_and_variance(u)

            first_stats(0)
            normalize(0, 1)
            for free in (oT_ready, x1_ready, *scores_free):
                dve.sem_inc(free, 1)
            weights.low(dve, nc.vector, WK, 0)
            xnT_low(0, 1)
            weights.low(dve, nc.vector, WK, 1)
            first_stats(1)
            for w, k in [(WK, 2), (WK, 3)] + [(WQ, k) for k in range(KB)]:
                weights.low(dve, nc.vector, w, k)
            normalize(1, 2)
            dve.wait_ge(table_loaded, 16)
            dve.wait_ge(k_in_psum, 1)
            rotate(k_ps, k_cos, k_sin, 0, k_rotated)
            for k in range(KB):
                weights.low(dve, nc.vector, WV, k)
            dve.wait_ge(q_in_psum, 1)
            rotate(q_ps, q_cos, q_sin, 0, q_rotated)
            xnT_low(1, 2)
            first_stats(2)
            dve.wait_ge(tables_loaded, 16)
            dve.wait_ge(consts_loaded, 16)
            dve.wait_ge(zeros_set, 1)

            dve.wait_ge(mixer.mu_loaded, 16)
            nc.vector.tensor_scalar(mixer.rest[:, :, :], mixer.mu[:, :, :], -1.0, 1.0, ALU.mult, ALU.add).then_inc(mixer.rest_ready, 1)
            nc.vector.memset(mixer.xT[:, :, 0:1], 0.0).then_inc(mixer.carried, 1)

            with dve.Fori(0, B - 1) as b:
                with dve.Fori(0, inner) as turn:
                    for u in range(UNROLL):
                        step(turn, b * per_batch + turn * UNROLL + u, b * inner + turn, u)
            norm.statistics(dve, 0, 16)
            dve.wait_ge(norm.stats_done, 1)
            norm.mean_and_variance()
            with dve.Fori(0, inner - 1) as turn:
                for u in range(UNROLL):
                    step(turn, (B - 1) * per_batch + turn * UNROLL + u, (B - 1) * inner + turn, u)
            for u in range(UNROLL):
                step(inner - 1, tiles - UNROLL + u, tiles // UNROLL - 1, u)

        @block.gpsimd
        def _(pool):
            def inverse_deviation(slot, count):
                pool.wait_ge(meanvar_ready, count)
                inverse_square_root(nc, pool, mean_var[slot][:, 1:2], [rstd[slot][:, i:i + 1] for i in range(4)],
                                    norm.power[:, 0:1], norm.epsilon[:, 0:1], norm.three_halves[:, 0:1],
                                    rstd_step, rstd_ready, count)

            def keys(count):
                pool.wait_ge(k_rotated, count)
                nc.gpsimd.tensor_tensor(k_sum[:], k_cos[:], k_sin[:], ALU.add).then_inc(k_summed, 1)

            def queries(count):
                pool.wait_ge(q_rotated, count)
                nc.gpsimd.tensor_tensor(q_sum[:], q_cos[:], q_sin[:], ALU.add).then_inc(q_summed, 1)

            def keys_low(slot, count):
                pool.wait_ge(k_hi_ready, count)
                nc.gpsimd.tensor_tensor(k_lo[:], k_nat[slot][:], k_hi[:].bitcast(F32), ALU.subtract).then_inc(k_split, 1)

            def step(tile, u):
                if within(tile, 2, tiles):
                    inverse_deviation(u % 2, tile + 3)
                if within(tile, 1, tiles):
                    pool.wait_ge(k_ready, tile + 1)
                    keys(tile + 2)
                    pool.wait_ge(q_ready, tile + 1)
                    queries(tile + 2)
                    keys_low((u + 1) % 2, tile + 2)

            pool.wait_ge(consts_set, 1)
            inverse_deviation(0, 1)
            inverse_deviation(1, 2)
            for i in range(2):
                nc.gpsimd.memset(qx_hi[i][:, :, :, :].bitcast(F32), 0.0)
                last = nc.gpsimd.memset(qx_lo[i][:, :, :, :].bitcast(F32), 0.0)
            last.then_inc(zeros_set, 1)
            nc.gpsimd.memset(carry[:].bitcast(F32), 0.0).then_inc(carry_ready, 1)
            keys(1)
            keys_low(0, 1)
            queries(1)
            pool.wait_ge(weights.lo_ready, 3 * KB)
            for k in range(KB):
                weights.low(pool, nc.gpsimd, WO, k)

            with pool.Fori(0, B - 1) as b:
                with pool.Fori(0, inner) as turn:
                    for u in range(UNROLL):
                        step(b * per_batch + turn * UNROLL + u, u)
            norm.inverse_deviation(pool, 1)
            with pool.Fori(0, inner - 1) as turn:
                for u in range(UNROLL):
                    step((B - 1) * per_batch + turn * UNROLL + u, u)
            for u in range(UNROLL):
                step(tiles - UNROLL + u, u)


def mix_phase(nc, sem, norm, weights, mixer, x1_dram, out, blocks_per_batch):
    N = blocks_per_batch
    blocks = x1_dram.shape[0] // T
    B = blocks // N
    x1_blocks = x1_dram.rearrange("(n j p) c -> n p j c", p=P, j=J)
    out_tiles = out.rearrange("b (n p) c -> (b n) p c", p=P)
    x1_sb, x1_loaded, xn, xn_ready = norm.x1, norm.x1_loaded, norm.xn, norm.xn_ready

    with ExitStack() as ctx:
        def sb(name, shape, dt=F32):
            return ctx.enter_context(nc.sbuf_tensor(name, shape, dt))

        w_hi, w_lo = weights.hi, weights.lo
        KEYS, RECEPTANCE, VALUES = FK % 4, FR % 4, FV % 4
        xT = mixer.xT
        mixer.part = [[sb(f"part{m}{i}", [P, T]) for i in range(2)] for m in range(2)]
        mixer.mixed = [[sb(f"mixed{m}{i}", [P, T]) for i in range(2)] for m in range(2)]
        mixer.m_hi[0], mixer.m_lo[0] = sb("m_hi0", [P, KB, T], F32R), sb("m_lo0", [P, KB, T], F32R)
        m_hi, m_lo, m_ready = mixer.m_hi, mixer.m_lo, mixer.m_ready
        k_relu = [sb(f"k_relu{i}", [P, T]) for i in range(2)]
        k_square = [sb(f"k_square{i}", [P, T]) for i in range(2)]
        ka_hi, ka_lo = sb("ka_hi", [P, KB, T], F32R), sb("ka_lo", [P, KB, T], F32R)
        gate = sb("gate", [P, J, C])
        gated = [sb(f"gated{i}", [P, C]) for i in range(2)]
        result = [sb(f"result{i}", [P, C]) for i in range(2)]

        xT_ps = [ctx.enter_context(nc.psum_tensor(f"xT_ps{i}", [P, 512], F32)) for i in range(2)]
        k_ps = [ctx.enter_context(nc.psum_tensor(f"f_k_ps{i}", [P, 512], F32)) for i in range(2)]
        xT_ps += k_ps
        r_ps = [ctx.enter_context(nc.psum_tensor(f"f_r_ps{i}", [P, 512], F32)) for i in range(2)]
        v_ps = [ctx.enter_context(nc.psum_tensor(f"f_v_ps{i}", [P, 512], F32)) for i in range(2)]

        def sems(name):
            return [sem(f"{name}{i}") for i in range(4)]
        k_in_psum, relu_done, square_done, ka_hi_ready, ka_ready = sems("f_k_in_psum"), sems("relu_done"), sems("square_done"), sems("ka_hi_ready"), sems("ka_ready")
        r_in_psum, gate_ready, v_in_psum, gated_ready, result_ready = sems("r_in_psum"), sems("gate_ready"), sems("f_v_in_psum"), sems("gated_ready"), sems("result_ready")
        stored = sems("stored")

        block = ctx.enter_context(nc.Block())

        def split3(psum, lhs_hi, lhs_lo, rhs_hi, rhs_lo, start, stop):
            nc.tensor.matmul(psum, lhs_hi, rhs_hi, start=start, stop=False)
            nc.tensor.matmul(psum, lhs_lo, rhs_hi, start=False, stop=False)
            return nc.tensor.matmul(psum, lhs_hi, rhs_lo, start=False, stop=stop)

        @block.sync
        def _(sp):
            def store(n, j):
                sp.wait_ge(result_ready[j], n + 1 + (j >= 2))
                sp.dma_start(out_tiles[bass.ds(n * J + j, 1), :, :].rearrange("o p c -> (o p) c"), result[j % 2][:]).then_inc(stored[j], 16)

            with sp.Fori(0, blocks // 2 - 1) as pair:
                for i in range(2):
                    n = pair * 2 + i
                    for j in range(J):
                        store(n, j)
                    sp.dma_start(x1_sb[i][:, :, :], x1_blocks[bass.ds(n + 2, 1), :, :, :].rearrange("o p j c -> (o p) j c")).then_inc(x1_loaded[i], 16)
            for i in range(2):
                for j in range(J):
                    store(blocks - 2 + i, j)
            for j in range(J):
                sp.wait_ge(stored[j], 16 * (blocks + (j >= 2)))

        @block.tensor
        def _(pe):
            def transposes(n):
                pe.wait_ge(xn_ready, n + 1)
                for k in range(KB):
                    if k >= 2:
                        pe.wait_ge(relu_done[k], n + 1)
                    for j in range(J):
                        last = nc.tensor.transpose(xT_ps[k][:, j * P:(j + 1) * P], xn[:, j, k * P:(k + 1) * P], norm.eye)
                    last.then_inc(mixer.xT_in_psum[k], 1)

            def step(n):
                for m in range(KB):
                    pe.wait_ge(relu_done[(m + 2) % 4], n + 1)
                    for k in range(KB):
                        if m == 0:
                            pe.wait_ge(m_ready[1][k], n + 1)
                        last = split3(k_ps[m % 2][:], w_hi[KEYS][:, k, m * P:(m + 1) * P], w_lo[KEYS][:, k, m * P:(m + 1) * P],
                                      m_hi[1][:, k, :], m_lo[1][:, k, :], k == 0, k == KB - 1)
                    last.then_inc(k_in_psum[m], 1)
                for j in range(J):
                    tok = slice(j * P, (j + 1) * P)
                    pe.wait_ge(gate_ready[(j + 2) % 4], n + 1)
                    if j == 0:
                        pe.wait_ge(weights.lo_ready, 7 * KB)
                    for k in range(KB):
                        if j == 0:
                            pe.wait_ge(m_ready[0][k], n + 1)
                        last = split3(r_ps[j % 2][:], m_hi[0][:, k, tok], m_lo[0][:, k, tok],
                                      w_hi[RECEPTANCE][:, k, :], w_lo[RECEPTANCE][:, k, :], k == 0, k == KB - 1)
                    last.then_inc(r_in_psum[j], 1)
                if within(n, 1, blocks):
                    transposes(n + 1)
                for j in range(J):
                    tok = slice(j * P, (j + 1) * P)
                    pe.wait_ge(gated_ready[(j + 2) % 4], n + 1 + (j >= 2))
                    for k in range(KB):
                        if j == 0:
                            pe.wait_ge(ka_ready[k], n + 1 + (k >= 2))
                        last = split3(v_ps[j % 2][:], ka_hi[:, k, tok], ka_lo[:, k, tok],
                                      w_hi[VALUES][:, k, :], w_lo[VALUES][:, k, :], k == 0, k == KB - 1)
                    last.then_inc(v_in_psum[j], 1)

            for i in (2, 3):
                pe.sem_inc(relu_done[i], 1)
                pe.sem_inc(gate_ready[i], 1)
            pe.wait_ge(weights.lo_ready, 5 * KB)
            with pe.Fori(0, B - 1) as b:
                for i in range(N):
                    step(b * N + i)
            for i in range(N):
                step(blocks - N + i)

        @block.scalar
        def _(act):
            def mix_keys(count):
                mixer.part_of_previous(act, 1, 0, count)
                for k in range(KB):
                    if k + 1 < KB:
                        mixer.part_of_previous(act, 1, k + 1, count)
                    mixer.high(act, 1, k, count)

            def step(n):
                mixer.part_of_previous(act, 0, 0, n + 1)
                for k in range(KB):
                    if k + 1 < KB:
                        mixer.part_of_previous(act, 0, k + 1, n + 1)
                    mixer.high(act, 0, k, n + 1)
                    act.wait_ge(k_in_psum[k], n + 1)
                    nc.scalar.activation(k_relu[k % 2][:], k_ps[k % 2][:], ACT.Relu).then_inc(relu_done[k], 1)
                    if k >= 1:
                        act.wait_ge(square_done[k - 1], n + 1)
                        nc.scalar.copy(ka_hi[:, k - 1, :], k_square[(k - 1) % 2][:]).then_inc(ka_hi_ready[k - 1], 1)
                act.wait_ge(square_done[KB - 1], n + 1)
                nc.scalar.copy(ka_hi[:, KB - 1, :], k_square[(KB - 1) % 2][:]).then_inc(ka_hi_ready[KB - 1], 1)
                for j in range(J):
                    act.wait_ge(r_in_psum[j], n + 1)
                    act.wait_ge(gated_ready[j], n + 1)
                    nc.scalar.activation(gate[:, j, :], r_ps[j % 2][:], ACT.Sigmoid).then_inc(gate_ready[j], 1)
                if within(n, 1, blocks):
                    for k in range(KB):
                        mixer.gather(act, xT_ps[k], k, n + 2)
                    mix_keys(n + 2)

            for k in range(KB):
                weights.high(act, FV, k)
            with act.Fori(0, B - 1) as b:
                for i in range(N):
                    step(b * N + i)
            for i in range(N):
                step(blocks - N + i)

        @block.vector
        def _(dve):
            def activation_low(k, count):
                dve.wait_ge(ka_hi_ready[k], count)
                nc.vector.tensor_tensor(ka_lo[:, k, :], k_square[k % 2][:], ka_hi[:, k, :].bitcast(F32),
                                        ALU.subtract).then_inc(ka_ready[k], 1)

            def apply_gate(j, n):
                dve.wait_ge(v_in_psum[j], n + 1)
                dve.wait_ge(gate_ready[j], n + 1 + (j >= 2))
                dve.wait_ge(result_ready[(j + 2) % 4], n + 1)
                nc.vector.tensor_tensor(gated[j % 2][:], v_ps[j % 2][:], gate[:, j, :], ALU.mult).then_inc(gated_ready[j], 1)

            def step(n, i, loads):
                mixer.mix(dve, 0, 0, n + 1)
                for k in range(KB):
                    if k + 1 < KB:
                        mixer.mix(dve, 0, k + 1, n + 1)
                    mixer.low(dve, 0, k, n + 1)
                    if 1 <= k < KB - 1:
                        activation_low(k - 1, n + 1)
                if not within(n, 1, blocks):
                    for k in (KB - 2, KB - 1):
                        activation_low(k, n + 1)
                    for j in range(J):
                        apply_gate(j, n)
                    return
                slot = (i + 1) % 2
                norm.statistics(dve, slot, loads)
                activation_low(KB - 2, n + 1)
                dve.wait_ge(norm.stats_done, n + 2)
                if i + 1 < N:
                    nc.vector.tensor_copy(xT[:, :, 0:1], xT[:, :, T:T + 1]).then_inc(mixer.carried, 1)
                else:
                    nc.vector.memset(xT[:, :, 0:1], 0.0).then_inc(mixer.carried, 1)
                norm.mean_and_variance()
                activation_low(KB - 1, n + 1)
                norm.normalize(dve, slot, n + 2)
                mixer.mix(dve, 1, 0, n + 2)
                mixer.mix(dve, 1, 1, n + 2)
                mixer.low(dve, 1, 0, n + 2)
                apply_gate(0, n)
                mixer.mix(dve, 1, 2, n + 2)
                mixer.low(dve, 1, 1, n + 2)
                apply_gate(1, n)
                mixer.mix(dve, 1, 3, n + 2)
                mixer.low(dve, 1, 2, n + 2)
                mixer.low(dve, 1, 3, n + 2)
                apply_gate(2, n)
                apply_gate(3, n)

            for j in range(J):
                dve.sem_inc(gated_ready[j], 1)
            for k in range(KB):
                weights.low(dve, nc.vector, FV, k)
            with dve.Fori(0, B - 1) as b:
                for i in range(N):
                    step(b * N + i, i, (b * (N // 2) + (i + 1) // 2) * 16 + 16)
            for i in range(N):
                step(blocks - N + i, i, ((B - 1) * (N // 2) + (i + 1) // 2) * 16 + 16)

        @block.gpsimd
        def _(pool):
            def step(n, i):
                for m in range(KB):
                    pool.wait_ge(relu_done[m], n + 1 + (m >= 2))
                    pool.wait_ge(ka_ready[(m + 2) % 4], n + 1)
                    nc.gpsimd.tensor_tensor(k_square[m % 2][:], k_relu[m % 2][:], k_relu[m % 2][:], ALU.mult).then_inc(square_done[m], 1)
                if within(n, 1, blocks):
                    norm.inverse_deviation(pool, n + 2)
                for j in range(J):
                    pool.wait_ge(gated_ready[j], n + 2)
                    pool.wait_ge(stored[(j + 2) % 4], n * 16 + 16)
                    nc.gpsimd.tensor_tensor(result[j % 2][:], gated[j % 2][:], x1_sb[i % 2][:, j, :], ALU.add).then_inc(result_ready[j], 1)

            for i in (2, 3):
                pool.sem_inc(ka_ready[i], 1)
                pool.sem_inc(result_ready[i], 1)
                pool.sem_inc(stored[i], 16)
            with pool.Fori(0, B - 1) as b:
                for i in range(N):
                    step(b * N + i, i)
            for i in range(N):
                step(blocks - N + i, i)


def layer(nc, x, wq, wk, wv, wo, w_r, w_k, w_v, mu, tables, consts, out):
    B, L, _ = x.shape
    x1_dram = nc.dram_tensor("x1_dram", [B * L, C], F32, kind="Internal").ap()
    with ExitStack() as ctx:
        def sem(name):
            return ctx.enter_context(nc.semaphore(name))

        weights = SplitWeights(ctx, nc, sem, [wk, wq, wv, wo, w_k, w_r, w_v])
        norm, mixer = BlockNorm(ctx, nc, sem), KeyMix(ctx, nc, sem)
        attention_phase(nc, sem, norm, weights, mixer, x, mu, tables, consts, x1_dram)
        mix_phase(nc, sem, norm, weights, mixer, x1_dram, out, L // 512)


def constants(length):
    theta = np.float32(10000.0)
    inv_freq = np.float32(1.0) / np.power(theta, np.arange(0, D, 2, dtype=np.float32) / np.float32(D), dtype=np.float32)
    angle = np.arange(length, dtype=np.float32)[:, None] * inv_freq[None, :]
    cos, sin = np.cos(angle), np.sin(angle)
    row = np.concatenate([np.repeat(cos, 2, axis=1), np.stack([-sin, sin], axis=-1).reshape(length, D)], axis=1)
    table = row.reshape(length // P, P, 2 * D).transpose(1, 0, 2)
    table = np.ascontiguousarray(np.concatenate([table, table[:, :1]], axis=1))
    at = np.arange(P)
    upto = (at[:, None] <= at[None, :]).astype(np.float32)
    carried = np.zeros((P, P), dtype=np.float32)
    carried[[3 * P // 4 - 1, P - 1]] = 1.0
    return {"tables": table, "consts": np.stack([np.eye(P, dtype=np.float32), upto, carried], axis=1)}


def kernel(L0_attn_x, L0_attn_wq, L0_attn_wk, L0_attn_wv, L0_attn_wo, L0_ffn_W_r, L0_ffn_W_k, L0_ffn_W_v,
           L0_ffn_mu_r, L0_ffn_mu_k):
    import concourse.bacc as bacc
    from concourse.bass_utils import run_bass_kernel_spmd

    x = np.asarray(L0_attn_x)
    arrays = {
        "x": x, "wq": np.asarray(L0_attn_wq), "wk": np.asarray(L0_attn_wk), "wv": np.asarray(L0_attn_wv),
        "wo": np.asarray(L0_attn_wo),
        "w_r": np.asarray(L0_ffn_W_r).T, "w_k": np.asarray(L0_ffn_W_k).T, "w_v": np.asarray(L0_ffn_W_v).T,
        "mu": np.stack([np.asarray(L0_ffn_mu_r), np.asarray(L0_ffn_mu_k)]).reshape(2, KB, P).transpose(2, 0, 1),
        **constants(x.shape[1]),
    }
    arrays = {name: np.ascontiguousarray(a) for name, a in arrays.items()}
    nc = bacc.Bacc("TRN2", target_bir_lowering=False, num_devices=1)
    ins = {name: nc.dram_tensor(f"in_{name}", a.shape, F32, kind="ExternalInput").ap() for name, a in arrays.items()}
    out = nc.dram_tensor("out", x.shape, F32, kind="ExternalOutput").ap()
    layer(nc, out=out, **ins)
    got = run_bass_kernel_spmd(nc, [{f"in_{name}": a for name, a in arrays.items()}], core_ids=[0])
    return got.results[0]["out"]
```
